# Optimizing a Trainium2 kernel written in Bass

```python
import numpy as np
import jax
import jax.numpy as jnp

def _softmax(x, axis=-1):
    return jax.nn.softmax(x, axis=axis)

def _gelu(x):
    return jax.nn.gelu(x, approximate=True)

def _silu(x):
    return jax.nn.silu(x)

def _sigmoid(x):
    return jax.nn.sigmoid(x)

def _layernorm(x, axis=-1, eps=1e-05):
    m = jnp.mean(x, axis=axis, keepdims=True)
    v = jnp.var(x, axis=axis, keepdims=True)
    return (x - m) / jnp.sqrt(v + eps)

def _scatter_add(tgt, idx, src, axis=0):
    return tgt.at[idx].add(src)

def _segment_sum(src, seg, n):
    return jax.ops.segment_sum(src, seg, n)
kernel_name = 'mk_cond_seq_d1_seqx_r2_598c37'

def setup_inputs(seed: int=0):
    np.random.seed(seed)
    _w = jnp.asarray

    def _rec_inputs():
        import jax
        import jax.numpy as jnp
        _rk = jax.random.key(seed)
        x = -0.0005207 + 1.001 * jax.random.normal(jax.random.fold_in(_rk, 1), (64, 128, 512), jnp.float32)
        _lenS = 128 - jax.random.randint(jax.random.fold_in(_rk, 7), (64,), 0, max(1, 128 // 4) + 1, jnp.int32)
        _lenS2 = 128 - jax.random.randint(jax.random.fold_in(_rk, 8), (64,), 0, max(1, 128 // 4) + 1, jnp.int32)
        itok_B_34_63 = jax.random.randint(jax.random.fold_in(_rk, 12), (64,), 34, 64, jnp.int32)
        fside_Bx16xSxS_0 = -1.47943e-05 + 1.00017 * jax.random.normal(jax.random.fold_in(_rk, 13), (64, 16, 128, 128), jnp.float32)
        _validS = jnp.arange(128)[None, :] < _lenS[:, None]
        _validS2 = jnp.arange(128)[None, :] < _lenS2[:, None]
        _causal = jnp.tril(jnp.ones((128, 128), dtype=bool))
        mask_Bx1xSxS_bk0 = jnp.logical_not(jnp.broadcast_to(_validS[:, None, None, :], (64, 1, 128, 128)))
        return (x, itok_B_34_63, fside_Bx16xSxS_0, mask_Bx1xSxS_bk0)
    x, itok_B_34_63, fside_Bx16xSxS_0, mask_Bx1xSxS_bk0 = _rec_inputs()

    def _L0_cond_setup():
        import jax, jax.numpy as jnp
        import numpy as np
        import math
        D_MODEL = 512
        N_HEAD = 16
        HEAD_DIM = D_MODEL // N_HEAD
        D_FF = 2048
        NUM_STEPS = 100.0
        RESCALE = 4000.0
        EPS = 1e-05

        def _sin_emb(t):
            half = D_MODEL // 2
            x = t.astype(jnp.float32) / NUM_STEPS * RESCALE
            freqs = jnp.exp(jnp.arange(half, dtype=jnp.float32) * (-math.log(10000.0) / (half - 1)))
            e = x[:, None] * freqs[None, :]
            return jnp.concatenate([jnp.sin(e), jnp.cos(e)], axis=-1)

        def _ln(x):
            m = jnp.mean(x, axis=-1, keepdims=True)
            v = jnp.var(x, axis=-1, keepdims=True)
            return (x - m) / jnp.sqrt(v + EPS)

        def _gelu2(x):
            return x * jax.nn.sigmoid(1.702 * x)
        key = jax.random.key(seed)
        ks = jax.random.split(key, 24)
        B, S, D, F = (4, 256, D_MODEL, D_FF)
        std = 0.02
        inp = {'src': jax.random.normal(ks[0], (B, S, D), dtype=jnp.float32), 'src_mask': jax.random.randint(ks[1], (B, 1, S, S), 0, 2).astype(bool), 'timestep': jax.random.randint(ks[2], (B,), 0, 100, dtype=jnp.int32), 'attention_bias': jax.random.normal(ks[3], (B, N_HEAD, S, S), dtype=jnp.float32), 'W_ada': jax.random.normal(ks[4], (D, 2 * D), dtype=jnp.float32) * std, 'b_ada': jnp.zeros((2 * D,), dtype=jnp.float32), 'Wq': jax.random.normal(ks[5], (D, D), dtype=jnp.float32) * std, 'bq': jnp.zeros((D,), dtype=jnp.float32), 'Wk': jax.random.normal(ks[6], (D, D), dtype=jnp.float32) * std, 'bk': jnp.zeros((D,), dtype=jnp.float32), 'Wv': jax.random.normal(ks[7], (D, D), dtype=jnp.float32) * std, 'bv': jnp.zeros((D,), dtype=jnp.float32), 'Wo': jax.random.normal(ks[8], (D, D), dtype=jnp.float32) * std, 'bo': jnp.zeros((D,), dtype=jnp.float32), 'W1': jax.random.normal(ks[9], (D, F), dtype=jnp.float32) * std, 'b1': jnp.zeros((F,), dtype=jnp.float32), 'W2': jax.random.normal(ks[10], (F, D), dtype=jnp.float32) * std, 'b2': jnp.zeros((D,), dtype=jnp.float32), 'g2': jnp.ones((D,), dtype=jnp.float32), 'beta2': jnp.zeros((D,), dtype=jnp.float32)}
        return inp
    _L0_cond_all = _L0_cond_setup()
    _L0_cond_in = {k: v for k, v in _L0_cond_all.items() if k in ('W_ada', 'b_ada', 'Wq', 'bq', 'Wk', 'bk', 'Wv', 'bv', 'Wo', 'bo', 'W1', 'b1', 'W2', 'b2', 'g2', 'beta2')}
    del _L0_cond_all
    return {'x': x, 'itok_B_34_63': itok_B_34_63, 'fside_Bx16xSxS_0': fside_Bx16xSxS_0, 'mask_Bx1xSxS_bk0': mask_Bx1xSxS_bk0, 'L0_cond_W_ada': _L0_cond_in['W_ada'], 'L0_cond_b_ada': _L0_cond_in['b_ada'], 'L0_cond_Wq': _L0_cond_in['Wq'], 'L0_cond_bq': _L0_cond_in['bq'], 'L0_cond_Wk': _L0_cond_in['Wk'], 'L0_cond_bk': _L0_cond_in['bk'], 'L0_cond_Wv': _L0_cond_in['Wv'], 'L0_cond_bv': _L0_cond_in['bv'], 'L0_cond_Wo': _L0_cond_in['Wo'], 'L0_cond_bo': _L0_cond_in['bo'], 'L0_cond_W1': _L0_cond_in['W1'], 'L0_cond_b1': _L0_cond_in['b1'], 'L0_cond_W2': _L0_cond_in['W2'], 'L0_cond_b2': _L0_cond_in['b2'], 'L0_cond_g2': _L0_cond_in['g2'], 'L0_cond_beta2': _L0_cond_in['beta2']}

def reference(x, itok_B_34_63, fside_Bx16xSxS_0, mask_Bx1xSxS_bk0, L0_cond_W_ada, L0_cond_b_ada, L0_cond_Wq, L0_cond_bq, L0_cond_Wk, L0_cond_bk, L0_cond_Wv, L0_cond_bv, L0_cond_Wo, L0_cond_bo, L0_cond_W1, L0_cond_b1, L0_cond_W2, L0_cond_b2, L0_cond_g2, L0_cond_beta2):
    import jax
    import jax.numpy as jnp

    def _L0_cond_ref(src, src_mask, timestep, attention_bias, W_ada, b_ada, Wq, bq, Wk, bk, Wv, bv, Wo, bo, W1, b1, W2, b2, g2, beta2):
        import jax, jax.numpy as jnp
        import numpy as np
        import math
        D_MODEL = 512
        N_HEAD = 16
        HEAD_DIM = D_MODEL // N_HEAD
        D_FF = 2048
        NUM_STEPS = 100.0
        RESCALE = 4000.0
        EPS = 1e-05

        def _sin_emb(t):
            half = D_MODEL // 2
            x = t.astype(jnp.float32) / NUM_STEPS * RESCALE
            freqs = jnp.exp(jnp.arange(half, dtype=jnp.float32) * (-math.log(10000.0) / (half - 1)))
            e = x[:, None] * freqs[None, :]
            return jnp.concatenate([jnp.sin(e), jnp.cos(e)], axis=-1)

        def _ln(x):
            m = jnp.mean(x, axis=-1, keepdims=True)
            v = jnp.var(x, axis=-1, keepdims=True)
            return (x - m) / jnp.sqrt(v + EPS)

        def _gelu2(x):
            return x * jax.nn.sigmoid(1.702 * x)
        B, S, D = src.shape
        emb = jax.nn.silu(_sin_emb(timestep)) @ W_ada + b_ada
        scale, shift = jnp.split(emb[:, None, :], 2, axis=-1)
        x = _ln(src) * (1.0 + scale) + shift
        q = (x @ Wq + bq).reshape(B, S, N_HEAD, HEAD_DIM).transpose(0, 2, 1, 3)
        k = (x @ Wk + bk).reshape(B, S, N_HEAD, HEAD_DIM).transpose(0, 2, 1, 3)
        v = (x @ Wv + bv).reshape(B, S, N_HEAD, HEAD_DIM).transpose(0, 2, 1, 3)
        scores = jnp.einsum('bhqd,bhkd->bhqk', q / math.sqrt(HEAD_DIM), k)
        scores = scores + attention_bias
        scores = jnp.where(src_mask, -jnp.inf, scores.astype(jnp.float32))
        probs = jax.nn.softmax(scores, axis=-1).astype(v.dtype)
        ctx = jnp.einsum('bhqk,bhkd->bhqd', probs, v)
        ctx = ctx.transpose(0, 2, 1, 3).reshape(B, S, D)
        x = x + (ctx @ Wo + bo)
        h = _ln(x) * g2 + beta2
        ff = _gelu2(h @ W1 + b1) @ W2 + b2
        return x + ff
    x = _L0_cond_ref(x, mask_Bx1xSxS_bk0, itok_B_34_63, fside_Bx16xSxS_0, L0_cond_W_ada, L0_cond_b_ada, L0_cond_Wq, L0_cond_bq, L0_cond_Wk, L0_cond_bk, L0_cond_Wv, L0_cond_bv, L0_cond_Wo, L0_cond_bo, L0_cond_W1, L0_cond_b1, L0_cond_W2, L0_cond_b2, L0_cond_g2, L0_cond_beta2)
    return x

_drawn_inputs = setup_inputs


def setup_inputs(seed=0):
    import zlib

    import numpy as np

    out = dict(_drawn_inputs(seed))
    spreads = {'L0_cond_b_ada': (0.0, 0.1),
     'L0_cond_bq': (0.0, 0.8),
     'L0_cond_bk': (0.0, 0.8),
     'L0_cond_bv': (0.0, 0.1),
     'L0_cond_bo': (0.0, 0.1),
     'L0_cond_b1': (0.0, 0.1),
     'L0_cond_b2': (0.0, 0.1),
     'L0_cond_g2': (1.0, 0.2),
     'L0_cond_beta2': (0.0, 0.36)}
    factors = {'L0_cond_Wq': 8.0, 'L0_cond_Wk': 8.0}
    for name, (base, spread) in spreads.items():
        noise = np.random.default_rng([zlib.crc32(name.encode()), seed]).standard_normal(out[name].shape)
        drawn = base * np.exp(spread * noise) if base else spread * noise
        out[name] = jnp.asarray(drawn.astype(out[name].dtype))
    for name, factor in factors.items():
        out[name] = (out[name] * factor).astype(out[name].dtype)
    return out
```

```python
import math
from collections import namedtuple
from contextlib import ExitStack

import numpy as np

import concourse.bass as bass
from concourse import mybir

F32 = mybir.dt.float32
F32R = mybir.dt.float32r
I32 = mybir.dt.int32
U8 = mybir.dt.uint8
ACT = mybir.ActivationFunctionType
ALU = mybir.AluOpType

P = 128
EPS = 1e-5
NUM_STEPS, RESCALE = 100.0, 4000.0
LOWEST = -3.0e38
ROUND = 1.5 * 2.0**23
TWO_PI = 2.0 * math.pi
PI_A = 6.28125
PI_B = float(np.float32(np.round((TWO_PI - PI_A) * 2**20) / 2**20))
PI_C = TWO_PI - PI_A - PI_B
DMA = 16


def at_least(eng, sem, count):
    if isinstance(count, int) and count <= 0:
        return
    eng.wait_ge(sem, count)


def variance(dve, st, part, mean, ve, stats_ok, done, var_ready, n, rows):
    even, odd, half = st[:, :, 0:3], st[:, :, 3:6], rows // 2
    at_least(dve, *stats_ok)
    dve.tensor_tensor(part[:, 0, :], even[:, :, 1], odd[:, :, 1], ALU.subtract)
    dve.tensor_tensor(part[:, 1, :], even[:, :, 2], odd[:, :, 2], ALU.add)
    dve.tensor_tensor(part[:, 2, :], even[:, :, 1], odd[:, :, 1], ALU.add).then_inc(done, 1)
    at_least(dve, done, n * 3 + 1)
    dve.tensor_tensor(part[:, 3, :], part[:, 0, :], part[:, 0, :], ALU.mult)
    dve.tensor_scalar(mean, part[:, 2, :], 0.5, None, ALU.mult).then_inc(done, 1)
    at_least(dve, done, n * 3 + 2)
    dve.scalar_tensor_tensor(out=part[:, 0, :], in0=part[:, 3, :], scalar=half / 2.0, in1=part[:, 1, :],
                             op0=ALU.mult, op1=ALU.add).then_inc(done, 1)
    at_least(dve, done, n * 3 + 3)
    dve.tensor_scalar(ve, part[:, 0, :], 1.0 / rows, EPS, ALU.mult, ALU.add).then_inc(var_ready, 1)


def setup_block(nc, d, w, adaT, ada_rows, ident, bq_s, bk_c, bv_bc, kbd):
    B, DM = d["x"].shape[0], d["x"].shape[2]
    HALF, CH, HD = DM // 2, DM // P, DM // 16
    with ExitStack() as ctx:
        sb = lambda name, shape, dt=F32: ctx.enter_context(nc.sbuf_tensor(name, shape, dt))
        sem = lambda name: ctx.enter_context(nc.semaphore(name))
        raw = [sb(f"raw_{n}", [P, CH, DM]) for n in ("q", "k", "v", "o")]
        w_ada = sb("w_ada", [P, CH, 2 * DM])
        b_ada = sb("b_ada", [B, 2 * DM])
        bo_bc = sb("bo_bc", [B, DM])
        bq_raw = sb("bq_raw", [P, CH])
        t_int = sb("t_int", [B, 1], I32)
        col = sb("col", [B, 8])
        q_hi = sb("q_hi", [B, 1], F32R)
        freqs = sb("freqs", [B, HALF])
        angle = sb("angle", [B, HALF])
        turns = sb("turns", [B, 2, HALF])
        rest = sb("rest", [B, 2, HALF])
        emb = sb("emb", [B, DM])
        expm = sb("expm", [B, DM])
        gate = sb("gate", [B, DM])
        embT = sb("embT", [P, CH, B])
        ada = sb("ada", [B, 2 * DM])
        rows = sb("rows", [B, 2 * DM])
        psT = ctx.enter_context(nc.psum_tensor("psT", [P, 2 * CH, B], F32))
        psA = ctx.enter_context(nc.psum_tensor("psA", [B, 2, DM], F32))
        small_in, ada_in, bias_in, w_in = sem("small_in"), sem("ada_in"), sem("row_bias_in"), [sem(f"w_in{i}") for i in range(4)]
        zeroed, ident_ok, step, sin_ok, exp_ok = sem("zeroed"), sem("ident_ok"), sem("step"), sem("sin_ok"), sem("exp_ok")
        turned, embT_ok, ada_ok, adaT_ok, rows_out, hi_ok = (
            sem("turned"), sem("embT_ok"), sem("ada_ok"), sem("adaT_ok"), sem("rows_out"), sem("hi_ok"))
        rest_ok, ada_sum, chain = sem("rest_ok"), sem("ada_sum"), sem("chain")
        block = ctx.enter_context(nc.Block())

        @block.sync
        def _(sp):
            sp.dma_start(t_int[:, :], d["t"].rearrange("(b a) -> b a", a=1)).then_inc(small_in, DMA)
            sp.dma_start(freqs[:, :], d["freqs"].rearrange("(a f) -> a f", a=1).to_broadcast([B, HALF])).then_inc(small_in, DMA)
            sp.dma_start(w_ada[:, :, :], d["W_ada"].rearrange("(c p) n -> p c n", p=P)).then_inc(ada_in, DMA)
            sp.dma_start(b_ada[:, :], d["b_ada"].rearrange("(a f) -> a f", a=1).to_broadcast([B, 2 * DM])).then_inc(bias_in, DMA)
            sp.dma_start(bo_bc[:, :], d["bo"].rearrange("(a f) -> a f", a=1).to_broadcast([B, DM])).then_inc(bias_in, DMA)
            sp.dma_start(bv_bc[:, :], d["bv"].rearrange("(a f) -> a f", a=1).to_broadcast([P, DM])).then_inc(bias_in, DMA)
            with nc.allow_non_contiguous_dma(reason="bias columns of 512 floats"):
                sp.dma_start(bq_raw[:, :], d["bq"].rearrange("(c p) -> p c", p=P)).then_inc(bias_in, DMA)
                sp.dma_start(bk_c[:, :], d["bk"].rearrange("(c p) -> p c", p=P)).then_inc(bias_in, DMA)
            for i, name in enumerate(("Wq", "Wk", "Wv", "Wo")):
                sp.dma_start(raw[i][:, :, :], d[name].rearrange("(c p) n -> p c n", p=P)).then_inc(w_in[i], DMA)
            sp.wait_ge(ada_sum, 3)
            sp.dma_start(ada_rows, rows[:, :]).then_inc(rows_out, DMA)
            sp.wait_ge(rows_out, DMA)

        @block.gpsimd
        def _(pool):
            pool.memset(ident[:, :], 0.0).then_inc(ident_ok, 1)
            pool.wait_ge(ident_ok, 1)
            pool.affine_select(out=ident[:, :], in_=ident[:, :], compare_op=ALU.not_equal, fill=1.0,
                               base=0, pattern=[[-1, P]], channel_multiplier=1).then_inc(ident_ok, 1)
            for t in kbd:
                pool.memset(t[:, :, :, :, :].bitcast(F32), 0.0).then_inc(zeroed, 1)
            pool.wait_ge(zeroed, len(kbd))

        @block.scalar
        def _(act):
            act.wait_ge(rest_ok, 1)
            act.activation(emb[:, :], rest[:, :, :].rearrange("b a f -> b (a f)"), ACT.Sin).then_inc(sin_ok, 1)
            act.wait_ge(sin_ok, 1)
            act.activation(expm[:, :], emb[:, :], ACT.Exp, scale=-1.0).then_inc(exp_ok, 1)
            for i in range(4):
                act.wait_ge(w_in[i], DMA)
                act.activation(w[i][0][:, :, :], raw[i][:, :, :], ACT.Copy).then_inc(hi_ok, 1)

        @block.tensor
        def _(pe):
            pe.wait_ge(ident_ok, 2)
            pe.wait_ge(step, 1)
            for c in range(CH):
                last = pe.transpose(psT[:, c, :], gate[:, c * P:(c + 1) * P], ident[0:B, 0:B])
            last.then_inc(turned, 1)
            pe.wait_ge(embT_ok, 1)
            pe.wait_ge(ada_in, DMA)
            for h in range(2):
                for c in range(CH):
                    last = pe.matmul(psA[:, h, :], embT[:, c, :], w_ada[:, c, h * DM:(h + 1) * DM],
                                     start=(c == 0), stop=(c == CH - 1))
            last.then_inc(ada_ok, 1)
            pe.wait_ge(ada_sum, 2)
            for c in range(2 * CH):
                last = pe.transpose(psT[:, c, :], ada[:, c * P:(c + 1) * P], ident[0:B, 0:B])
            last.then_inc(turned, 1)

        @block.vector
        def _(dve):
            count = [0]

            def then(ins):
                count[0] += 1
                ins.then_inc(chain, 1)
                dve.wait_ge(chain, count[0])

            dve.wait_ge(small_in, 2 * DMA)
            then(dve.tensor_copy(col[:, 0:1], t_int[:, :]))
            then(dve.tensor_scalar(col[:, 1:2], col[:, 0:1], 1.0 / NUM_STEPS, None, ALU.mult))
            then(dve.tensor_copy(q_hi[:, :], col[:, 1:2]))
            then(dve.tensor_tensor(col[:, 2:3], col[:, 1:2], q_hi[:, :].bitcast(F32), ALU.subtract))
            then(dve.scalar_tensor_tensor(out=col[:, 3:4], in0=q_hi[:, :].bitcast(F32), scalar=-NUM_STEPS,
                                          in1=col[:, 0:1], op0=ALU.mult, op1=ALU.add))
            then(dve.scalar_tensor_tensor(out=col[:, 4:5], in0=col[:, 2:3], scalar=-NUM_STEPS,
                                          in1=col[:, 3:4], op0=ALU.mult, op1=ALU.add))
            then(dve.scalar_tensor_tensor(out=col[:, 5:6], in0=col[:, 4:5], scalar=1.0 / NUM_STEPS,
                                          in1=col[:, 1:2], op0=ALU.mult, op1=ALU.add))
            then(dve.tensor_scalar(col[:, 6:7], col[:, 5:6], RESCALE, None, ALU.mult))
            then(dve.tensor_scalar(angle[:, :], freqs[:, :], col[:, 6:7], None, ALU.mult))
            for a, quarter in enumerate((0.0, 0.25)):
                k, r = turns[:, a, :], rest[:, a, :]
                then(dve.tensor_scalar(k, angle[:, :], 1.0 / TWO_PI, quarter, ALU.mult, ALU.add))
                then(dve.tensor_scalar(k, k, ROUND, None, ALU.add))
                then(dve.tensor_scalar(k, k, ROUND, None, ALU.subtract))
                then(dve.scalar_tensor_tensor(out=r, in0=k, scalar=-PI_A, in1=angle[:, :], op0=ALU.mult, op1=ALU.add))
                then(dve.scalar_tensor_tensor(out=r, in0=k, scalar=-PI_B, in1=r, op0=ALU.mult, op1=ALU.add))
                then(dve.scalar_tensor_tensor(out=r, in0=k, scalar=-PI_C, in1=r, op0=ALU.mult, op1=ALU.add))
                if quarter:
                    then(dve.tensor_scalar(r, r, TWO_PI * quarter, None, ALU.add))
            dve.tensor_scalar(rest[:, :, :], rest[:, :, :], 3.1415925, -3.1415925, ALU.min, ALU.max).then_inc(rest_ok, 1)
            dve.wait_ge(exp_ok, 1)
            then(dve.tensor_scalar(expm[:, :], expm[:, :], 1.0, None, ALU.add))
            then(dve.reciprocal(expm[:, :], expm[:, :]))
            dve.tensor_tensor(gate[:, :], emb[:, :], expm[:, :], ALU.mult).then_inc(step, 1)
            dve.wait_ge(bias_in, 5 * DMA)
            dve.tensor_scalar(bq_s[:, :], bq_raw[:, :], HD ** -0.5, None, ALU.mult)
            dve.wait_ge(turned, 1)
            dve.tensor_copy(embT[:, :, :], psT[:, 0:CH, :]).then_inc(embT_ok, 1)
            dve.wait_ge(ada_ok, 1)
            dve.scalar_tensor_tensor(out=ada[:, 0:DM], in0=psA[:, 0, :], scalar=1.0, in1=b_ada[:, 0:DM],
                                     op0=ALU.add, op1=ALU.add).then_inc(ada_sum, 1)
            dve.tensor_tensor(ada[:, DM:], psA[:, 1, :], b_ada[:, DM:], ALU.add).then_inc(ada_sum, 1)
            dve.wait_ge(ada_sum, 2)
            then(dve.tensor_copy(rows[:, 0:DM], ada[:, 0:DM]))
            dve.tensor_tensor(rows[:, DM:], ada[:, DM:], bo_bc[:, :], ALU.add).then_inc(ada_sum, 1)
            dve.wait_ge(turned, 2)
            dve.tensor_copy(adaT[:, :, :], psT[:, :, :]).then_inc(adaT_ok, 1)
            for i in range(4):
                dve.wait_ge(hi_ok, i + 1)
                dve.tensor_tensor(w[i][1][:, :, :], raw[i][:, :, :], w[i][0][:, :, :].bitcast(F32), ALU.subtract)


Stages = namedtuple("Stages", "attn prev proj norm")


def stages(p, pairs):
    there = lambda q: 0 <= q < pairs
    return Stages(there(p), there(p - 1), there(p + 1), there(p + 2))


def attention_block(nc, d, w, adaT, ada_rows, resid, ident, bq_s, bk_c, bv_bc, kbd):
    B, S, DM = d["x"].shape
    H = d["bias"].shape[1]
    HD, CH = DM // H, DM // P
    HG = P // HD
    G = H // HG
    PAIRS, SLOTS = B // 2, 2 * G
    wq, wk, wv, wo = w
    with ExitStack() as ctx:
        sb = lambda name, shape, dt=F32: ctx.enter_context(nc.sbuf_tensor(name, shape, dt))
        sem = lambda name: ctx.enter_context(nc.semaphore(name))
        xin = sb("xin", [P, 2, DM])
        xn = sb("xn", [P, 2, DM])
        xres = sb("xres", [P, 2, 2, DM])
        st, part, mean, ve, rstd, expo = sb("st", [P, 2, 6]), sb("part", [P, 4, 2]), sb("mean", [P, 2]), sb("ve", [P, 2]), sb("rstd", [P, 2]), sb("expo", [P, 2])
        adab = sb("adab", [P, 2, 2 * DM])
        xTf = sb("xTf", [P, CH, P])
        xT = [sb(f"xT_{n}", [P, CH, 2 * P], F32R) for n in ("hi", "lo")]
        kf, qf = sb("kf", [P, 2, 2 * P]), sb("qf", [P, 2, 2 * P])
        qT = [sb(f"qT_{n}", [P, G, 2 * P], F32R) for n in ("hi", "lo")]
        kT = sb("kT", [P, 2, G, 2 * P], F32R)
        v = sb("v", [P, 2, 2, DM])
        bias = sb("bias", [P, 2, H, S])
        mask = sb("mask", [P, 2, S], U8)
        mneg = sb("mneg", [P, 2, S])
        s = sb("s", [P, 2, HG, S])
        mx, nmx = sb("mx", [P, 2, HG]), sb("nmx", [P, 2, HG])
        sums, rinv = sb("sums", [P, 2, HG]), sb("rinv", [P, 2, HG])
        pT = sb("pT", [P, 2, HG, P])
        cT = [sb(f"cT_{n}", [P, G, P], F32R) for n in ("hi", "lo")]
        rout = sb("rout", [P, 2, DM])
        psS = [ctx.enter_context(nc.psum_tensor(f"psS{i}", [P, HG, S], F32)) for i in range(2)]
        psP = [ctx.enter_context(nc.psum_tensor(f"psP{i}", [P, HG, P], F32)) for i in range(2)]
        psD = [ctx.enter_context(nc.psum_tensor(f"psD{i}", [P, DM], F32)) for i in range(2)]
        psC = ctx.enter_context(nc.psum_tensor("psC", [P, G, P], F32))
        psX = ctx.enter_context(nc.psum_tensor("psX", [P, CH, P], F32))
        x_in, adab_in = sem("x_in"), sem("adab_in")
        bias_in = [sem(f"bias_in{b}") for b in range(2)]
        kbd_in = [sem(f"kbd_in{b}") for b in range(2)]
        r_out = [sem(f"r_out{b}") for b in range(2)]
        expo_ok, bn_done, part_done, var_ready, rstd_ready, xn_ready = (
            sem("expo_ok"), sem("bn_done"), sem("part_done"), sem("var_ready"), sem("rstd_ready"), sem("xn_ready"))
        xt_done, xt_copied, x_hi, x_split = sem("xt_done"), sem("xt_copied"), sem("x_hi"), sem("x_split")
        res_half, res_ready = sem("res_half"), sem("res_ready")
        v_done, v_ready = sem("v_done"), sem("v_ready")
        k_done, k_copied, k_hi, k_split = sem("k_done"), sem("k_copied"), sem("k_hi"), sem("k_split")
        q_done, q_copied, q_hi, q_split = sem("q_done"), sem("q_copied"), sem("q_hi"), sem("q_split")
        mask_in = [sem(f"mask_in{b}") for b in range(2)]
        neg_ready = [sem(f"neg_ready{b}") for b in range(2)]
        bias_ready = [sem(f"bias_ready{b}") for b in range(2)]
        qk_done, score_ready, max_done, nmax_ready, exp_done = sem("qk_done"), sem("score_ready"), sem("max_done"), sem("nmax_ready"), sem("exp_done")
        rinv_ready, prob_ready = sem("rinv_ready"), sem("prob_ready")
        pt_done, pt_copied, pv_done = sem("pt_done"), sem("pt_copied"), sem("pv_done")
        ctx_hi, ctx_split, o_done, r_ready = sem("ctx_hi"), sem("ctx_split"), sem("o_done"), sem("r_ready")
        block = ctx.enter_context(nc.Block())

        x_rows = d["x"].rearrange("b s n -> s b n")
        bias_rows = d["bias"].rearrange("b h q k -> q b h k")
        mask_rows = d["mask"].rearrange("b a q k -> q b (a k)")
        r_rows = resid.rearrange("b s n -> s b n")

        def run(eng, step):
            first, last = 2, PAIRS - 3
            for p in range(-2, first):
                step(p, p % 2, stages(p, PAIRS))
            with eng.Fori(0, (last - first + 1) // 2) as i:
                for u in range(2):
                    step(i * 2 + (first + u), u, Stages(True, True, True, True))
            for p in range(last + 1, PAIRS + 1):
                step(p, p % 2, stages(p, PAIRS))

        @block.sync
        def _(sp):
            def load_bias(q, b):
                at_least(sp, score_ready, (q - 1) * SLOTS + (G * b + G))
                for half in (slice(0, H // 2), slice(H // 2, H)):
                    sp.dma_start(bias[:, b, half, :], bias_rows[:, bass.ds(q * 2 + b, 1), half, :]).then_inc(bias_in[b], DMA)
                sp.dma_start(mask[:, b, :], mask_rows[:, bass.ds(q * 2 + b, 1), :]).then_inc(mask_in[b], DMA)

            def spread_k(q, b):
                at_least(sp, k_split, q * G + G)
                at_least(sp, qk_done, (q - 1) * SLOTS + (G * b + G))
                for j in range(HG):
                    rows = slice(HD * j, HD * j + HD)
                    sp.dma_start(kbd[b][rows, :, :, j, :].bitcast(F32), kT[rows, :, :, b * P:(b + 1) * P].bitcast(F32)).then_inc(kbd_in[b], DMA)

            def store(q, b):
                at_least(sp, r_ready, q * 2 + (b + 1))
                sp.dma_start(r_rows[:, bass.ds(q * 2 + b, 1), :], rout[:, b, :]).then_inc(r_out[b], DMA)

            def step(p, u, on):
                if on.attn:
                    load_bias(p, 1)
                    spread_k(p, 1)
                if on.norm:
                    at_least(sp, xn_ready, p * 2 + 4)
                    sp.dma_start(xin[:, :, :], x_rows[:, bass.ds(p * 2 + 4, 2), :]).then_inc(x_in, DMA)
                if on.proj:
                    at_least(sp, res_ready, p * 2 + 2)
                    sp.dma_start(adab[:, :, :], ada_rows[bass.ds(p * 2 + 2, 2), :].unsqueeze(0)
                                 .to_broadcast([P, 2, 2 * DM])).then_inc(adab_in, DMA)
                if on.prev:
                    store(p - 1, 0)
                if on.proj:
                    load_bias(p + 1, 0)
                    spread_k(p + 1, 0)
                if on.prev:
                    store(p - 1, 1)

            run(sp, step)
            for b in range(2):
                sp.wait_ge(r_out[b], DMA * PAIRS)

        @block.gpsimd
        def _(pool):
            def add_mask(q, b, g):
                at_least(pool, bias_in[b], (q + 1) * (2 * DMA))
                at_least(pool, neg_ready[b], q + 1)
                heads = slice(HG * g, HG * g + HG)
                pool.tensor_tensor(bias[:, b, heads, :], bias[:, b, heads, :],
                                   mneg[:, b, :].unsqueeze(1).to_broadcast([P, HG, S]), ALU.add).then_inc(bias_ready[b], 1)

            def normalize_p(t, i):
                at_least(pool, rinv_ready, t + 1)
                pool.tensor_tensor(s[:, i, :, :], s[:, i, :, :], rinv[:, i, :].unsqueeze(2).to_broadcast([P, HG, S]),
                                   ALU.mult).then_inc(prob_ready, 1)

            def residual(q, u, b, prev):
                at_least(pool, xn_ready, q * 2 + (b + 1))
                at_least(pool, adab_in, (q + 1) * DMA)
                if prev:
                    at_least(pool, r_ready, (q - 2) * 2 + (b + 1))
                pool.tensor_tensor(xres[:, u, b, :], xn[:, b, :], adab[:, b, 0:DM], ALU.mult).then_inc(res_half, 1)
                at_least(pool, res_half, q * 2 + (b + 1))
                pool.tensor_tensor(xres[:, u, b, :], xres[:, u, b, :], adab[:, b, DM:], ALU.add).then_inc(res_ready, 1)

            def step(p, u, on):
                for n in range(SLOTS):
                    b, g = n // G, n % G
                    if on.attn and n or on.prev and n == 0:
                        normalize_p(p * SLOTS + n - 1, (g - 1) % 2)
                    if g == 0 and on.attn:
                        add_mask(p, b, G - 1)
                    if g and b == 0 and on.attn:
                        add_mask(p, 1, g - 1)
                    if g and b == 1 and on.proj:
                        add_mask(p + 1, 0, g - 1)
                    if n in (3, 5) and on.proj:
                        residual(p + 1, 1 - u, n // 4, on.prev)
                    if n == 6 and on.norm:
                        at_least(pool, var_ready, p + 3)
                        pool.tensor_tensor(rstd[:, :], ve[:, :], expo[:, :], ALU.pow).then_inc(rstd_ready, 1)

            pool.memset(expo[:, :], -0.5).then_inc(expo_ok, 1)
            pool.wait_ge(expo_ok, 1)
            run(pool, step)

        @block.scalar
        def _(act):
            def copy_xT(q, b):
                at_least(act, xt_done, q * 2 + (b + 1))
                at_least(act, x_split, q * 2 + b)
                at = bass.ds(q * 2 + b, 1)
                for c in range(CH):
                    last = act.activation(xTf[:, c, :], psX[:, c, :], ACT.Identity,
                                          scale=adaT[:, c, at], bias=adaT[:, CH + c, at])
                last.then_inc(xt_copied, 1)

            def copy_k(q, g):
                at_least(act, k_done, q * G + (g + 1))
                at_least(act, k_split, q * G + (g - 1))
                act.activation(kf[:, g % 2, :], psD[g % 2][:, 0:2 * P], ACT.Identity,
                               bias=bk_c[:, g:g + 1]).then_inc(k_copied, 1)

            def copy_q(q, g):
                at_least(act, q_done, q * G + (g + 1))
                at_least(act, q_split, q * G + (g - 1))
                act.activation(qf[:, g % 2, :], psD[(g + 1) % 2 if g < 2 else 1][:, 0:2 * P], ACT.Identity,
                               bias=bq_s[:, g:g + 1], scale=HD ** -0.5).then_inc(q_copied, 1)

            def copy_pT(t, i):
                at_least(act, pt_done, t + 1)
                at_least(act, pv_done, t - 1)
                act.activation(pT[:, i, :, :], psP[i][:, :, :], ACT.Copy).then_inc(pt_copied, 1)

            def exps(t, g):
                at_least(act, nmax_ready, t + 1)
                for j in range(HG):
                    last = act.activation(s[:, g % 2, j, :], s[:, g % 2, j, :], ACT.Exp,
                                          bias=nmx[:, g % 2, j:j + 1], accum_out=sums[:, g % 2, j:j + 1])
                last.then_inc(exp_done, 1)

            def step(p, u, on):
                for n in range(SLOTS):
                    b, g = n // G, n % G
                    t = p * SLOTS + n
                    if n < 2 and on.prev or n >= 2 and on.attn:
                        copy_pT(t - 2, g % 2)
                    if on.proj and n < 2:
                        copy_xT(p + 1, n)
                    if on.proj and n in (2, 3):
                        copy_k(p + 1, 2 * n - 4)
                    if on.proj and n in (5, 6):
                        copy_q(p + 1, 2 * n - 10)
                    if on.attn:
                        exps(t, g)
                    if on.proj and n in (2, 3):
                        copy_k(p + 1, 2 * n - 3)
                    if on.proj and n in (5, 7):
                        copy_q(p + 1, n - 4)

            run(act, step)

        @block.vector
        def _(dve):
            def split(hi, lo, of, hi_sem, done, n):
                dve.tensor_copy(hi, of).then_inc(hi_sem, 1)
                at_least(dve, hi_sem, n + 1)
                dve.tensor_tensor(lo, of, hi.bitcast(F32), ALU.subtract).then_inc(done, 1)

            def split_x(q, b):
                at_least(dve, xt_copied, q * 2 + (b + 1))
                at_least(dve, q_done, q * G)
                at = slice(b * P, (b + 1) * P)
                split(xT[0][:, :, at], xT[1][:, :, at], xTf[:, :, :], x_hi, x_split, q * 2 + b)

            def split_k(q, g):
                at_least(dve, k_copied, q * G + (g + 1))
                at_least(dve, kbd_in[1], q * (HG * DMA))
                split(kT[:, 0, g, :], kT[:, 1, g, :], kf[:, g % 2, :], k_hi, k_split, q * G + g)

            def split_q(q, g):
                at_least(dve, q_copied, q * G + (g + 1))
                at_least(dve, qk_done, (q - 1) * SLOTS + (G + g + 1))
                split(qT[0][:, g, :], qT[1][:, g, :], qf[:, g % 2, :], q_hi, q_split, q * G + g)

            def add_bv(q, u, b):
                at_least(dve, v_done, q * 2 + (b + 1))
                at_least(dve, pv_done, (q - 2) * SLOTS + (G * b + G))
                dve.tensor_tensor(v[:, u, b, :], psD[1 - b][:, :], bv_bc[:, :], ALU.add).then_inc(v_ready, 1)

            def scores(p, t, b, g):
                at_least(dve, qk_done, t + 1)
                at_least(dve, bias_ready[b], p * G + (g + 1))
                at_least(dve, pt_done, t - 1)
                dve.tensor_tensor(s[:, g % 2, :, :], psS[g % 2][:, :, :], bias[:, b, HG * g:HG * g + HG, :],
                                  ALU.add).then_inc(score_ready, 1)
                at_least(dve, score_ready, t + 1)
                dve.tensor_reduce(mx[:, g % 2, :], s[:, g % 2, :, :], mybir.AxisListType.X, ALU.max).then_inc(max_done, 1)
                at_least(dve, max_done, t + 1)
                dve.tensor_scalar(nmx[:, g % 2, :], mx[:, g % 2, :], -1.0, None, ALU.mult).then_inc(nmax_ready, 1)

            def invert(t, i):
                at_least(dve, exp_done, t + 1)
                at_least(dve, prob_ready, t - 1)
                dve.reciprocal(rinv[:, i, :], sums[:, i, :]).then_inc(rinv_ready, 1)

            def negate_mask(q, b):
                at_least(dve, mask_in[b], (q + 1) * DMA)
                at_least(dve, bias_ready[b], q * G)
                dve.tensor_scalar(mneg[:, b, :], mask[:, b, :], LOWEST, None, ALU.mult).then_inc(neg_ready[b], 1)

            def context(q, b):
                at_least(dve, pv_done, q * SLOTS + (G * b + G))
                at_least(dve, o_done, q * 2 + b)
                split(cT[0][:, :, :], cT[1][:, :, :], psC[:, :, :], ctx_hi, ctx_split, q * 2 + b)

            def add_residual(q, u, b):
                at_least(dve, o_done, q * 2 + (b + 1))
                at_least(dve, res_ready, q * 2 + (b + 1))
                at_least(dve, r_out[b], q * DMA)
                dve.tensor_tensor(rout[:, b, :], psD[0][:, :], xres[:, u, b, :], ALU.add).then_inc(r_ready, 1)

            def statistics(q):
                at_least(dve, x_in, (q + 1) * DMA)
                at_least(dve, xn_ready, q * 2)
                for b in range(2):
                    dve.bn_stats(st[:, b, :], xin[:, b, :]).then_inc(bn_done, 1)
                at_least(dve, rstd_ready, q)
                variance(dve, st, part, mean[:, :], ve[:, :], (bn_done, q * 2 + 2), part_done, var_ready, q, DM)

            def normalize(q, b):
                at_least(dve, rstd_ready, q + 1)
                at_least(dve, xt_done, q * 2)
                at_least(dve, res_ready, q * 2)
                dve.tensor_scalar(xn[:, b, :], xin[:, b, :], mean[:, b:b + 1], rstd[:, b:b + 1],
                                  ALU.subtract, ALU.mult).then_inc(xn_ready, 1)

            def step(p, u, on):
                for n in range(SLOTS):
                    b, g = n // G, n % G
                    t = p * SLOTS + n
                    if on.attn and n or on.prev and n == 0:
                        invert(t - 1, (g - 1) % 2)
                    if n == 0 and on.attn:
                        split_q(p, 3)
                    if n == 1 and on.prev:
                        add_residual(p - 1, 1 - u, 0)
                    if n == 2 and on.proj:
                        add_bv(p + 1, 1 - u, 0)
                    if n == 5 and on.prev:
                        add_residual(p - 1, 1 - u, 1)
                    if on.attn:
                        scores(p, t, b, g)
                    if n == 0 and on.attn:
                        negate_mask(p, 1)
                    if n == 4 and on.proj:
                        negate_mask(p + 1, 0)
                    if n < 2 and on.proj:
                        split_x(p + 1, n)
                    if n == 2 and on.prev:
                        context(p - 1, 1)
                    if n == 6 and on.attn:
                        context(p, 0)
                    if on.proj:
                        for gg in {3: (0, 1), 4: (2, 3)}.get(n, ()):
                            split_k(p + 1, gg)
                        for gg in {5: (0,), 6: (1,), 7: (2,)}.get(n, ()):
                            split_q(p + 1, gg)
                    if n == 5 and on.norm:
                        statistics(p + 2)
                    if n == 7 and on.norm:
                        normalize(p + 2, 0)
                    if n == 7 and on.proj:
                        add_bv(p + 1, 1 - u, 1)
                    if n == 7 and on.norm:
                        normalize(p + 2, 1)

            run(dve, step)

        @block.tensor
        def _(pe):
            def three(out, stat, moving, start, stop):
                (sh, sl), (mh, ml) = stat, moving
                pe.matmul(out, sh, mh, start=start, stop=False)
                pe.matmul(out, sh, ml, start=False, stop=False)
                return pe.matmul(out, sl, mh, start=False, stop=stop)

            def transpose_x(q, b):
                at_least(pe, xn_ready, q * 2 + (b + 1))
                for c in range(CH):
                    last = pe.transpose(psX[:, c, :], xn[:, b, c * P:(c + 1) * P], ident[:, :])
                last.then_inc(xt_done, 1)

            def qk(p, t, b, g):
                at_least(pe, score_ready, t - 1)
                if g == 0:
                    at_least(pe, kbd_in[b], (p + 1) * (HG * DMA))
                if b == 0:
                    at_least(pe, q_split, p * G + (g + 1))
                at = slice(b * P, (b + 1) * P)
                three(psS[g % 2][:, :, :], [x[:, g, at] for x in qT], [kbd[b][:, i, g, :, :] for i in range(2)],
                      True, True).then_inc(qk_done, 1)

            def transpose_p(t, i):
                at_least(pe, prob_ready, t + 1)
                at_least(pe, pt_copied, t - 1)
                for j in range(HG):
                    last = pe.transpose(psP[i][:, j, :], s[:, i, j, :], ident[:, :])
                last.then_inc(pt_done, 1)

            def pv(q, t, u, b, g):
                at_least(pe, pt_copied, t + 1)
                if g == 0:
                    at_least(pe, v_ready, q * 2 + (b + 1))
                    at_least(pe, ctx_split, q * 2 + b)
                for j in range(HG):
                    h = HG * g + j
                    last = pe.matmul(psC[HD * j:HD * j + HD, g, :], v[:, u, b, h * HD:(h + 1) * HD],
                                     pT[:, g % 2, j, :], start=True, stop=True, tile_position=(0, HD * j))
                last.then_inc(pv_done, 1)

            def project_v(q, b, chunks):
                if chunks[0] == 0:
                    at_least(pe, x_split, q * 2 + (b + 1))
                at = slice(b * P, (b + 1) * P)
                for c in chunks:
                    last = three(psD[1 - b][:, :], [x[:, c, at] for x in xT], [m[:, c, :] for m in wv],
                                 c == 0, c == CH - 1)
                if chunks[-1] == CH - 1:
                    last.then_inc(v_done, 1)

            def project_t(q, g, wm, bank, done):
                if g == 0:
                    at_least(pe, x_split, q * 2 + 2)
                for c in range(CH):
                    last = three(psD[bank][:, 0:2 * P], [m[:, c, g * P:(g + 1) * P] for m in wm],
                                 [x[:, c, :] for x in xT], c == 0, c == CH - 1)
                last.then_inc(done, 1)

            def project_o(q, b):
                at_least(pe, ctx_split, q * 2 + (b + 1))
                for c in range(CH):
                    last = three(psD[0][:, :], [x[:, c, :] for x in cT], [m[:, c, :] for m in wo], c == 0, c == CH - 1)
                last.then_inc(o_done, 1)

            def dense(p, n, on):
                q = p + 1
                if n == 0:
                    if on.proj:
                        at_least(pe, xt_copied, q * 2)
                        transpose_x(q, 0)
                    if on.prev:
                        if on.attn:
                            at_least(pe, v_ready, p * 2 + 2)
                        else:
                            at_least(pe, r_ready, p * 2 - 2)
                        project_o(p - 1, 0)
                    if on.proj:
                        at_least(pe, xt_copied, q * 2 + 1)
                        transpose_x(q, 1)
                if n == 1 and on.proj:
                    at_least(pe, q_copied, p * G + G)
                    project_v(q, 0, range(CH))
                if n == 2 and on.proj:
                    if on.prev:
                        at_least(pe, r_ready, p * 2 - 1)
                    else:
                        at_least(pe, v_ready, p * 2 + 2)
                    project_t(q, 0, wk, 0, k_done)
                    at_least(pe, v_ready, q * 2 + 1)
                    project_t(q, 1, wk, 1, k_done)
                if n == 3 and on.proj:
                    at_least(pe, k_copied, q * G + 1)
                    project_t(q, 2, wk, 0, k_done)
                    at_least(pe, k_copied, q * G + 2)
                    project_t(q, 3, wk, 1, k_done)
                if n == 4 and on.prev:
                    if on.proj:
                        at_least(pe, k_copied, q * G + 3)
                    else:
                        at_least(pe, r_ready, p * 2 - 1)
                    project_o(p - 1, 1)
                if n == 5 and on.proj:
                    at_least(pe, k_copied, q * G + 4)
                    project_t(q, 0, wq, 1, q_done)
                    if on.prev:
                        at_least(pe, r_ready, p * 2)
                    else:
                        at_least(pe, k_copied, q * G + 3)
                    project_t(q, 1, wq, 0, q_done)
                if n == 6 and on.proj:
                    at_least(pe, q_copied, q * G + 1)
                    project_t(q, 2, wq, 1, q_done)
                    at_least(pe, q_copied, q * G + 2)
                    project_v(q, 1, range(CH // 2))
                if n == 7 and on.proj:
                    project_v(q, 1, range(CH // 2, CH))
                    at_least(pe, q_copied, q * G + 3)
                    project_t(q, 3, wq, 1, q_done)

            def step(p, u, on):
                for n in range(SLOTS):
                    b, g = n // G, n % G
                    t = p * SLOTS + n
                    if on.attn:
                        qk(p, t, b, g)
                    dense(p, n, on)
                    if on.attn and n or on.prev and n == 0:
                        transpose_p(t - 1, (g - 1) % 2)
                    if n == 1 and on.prev:
                        for g in (G - 2, G - 1):
                            pv(p - 1, t - 1 - G + g, 1 - u, 1, g)
                    if n in (3, 5, 7) and on.attn:
                        for m in (n - 3, n - 2):
                            pv(p, p * SLOTS + m, u, m // G, m % G)

            run(pe, step)


def feed_block(nc, d, resid, ident, out):
    B, S, DM = d["x"].shape
    FF = d["W1"].shape[1]
    CH, J = DM // P, FF // P
    NB = 4
    GROUPS, ROWS = B // NB, NB * P
    with ExitStack() as ctx:
        sb = lambda name, shape, dt=F32: ctx.enter_context(nc.sbuf_tensor(name, shape, dt))
        sem = lambda name: ctx.enter_context(nc.semaphore(name))
        w1 = [sb(f"w1_{n}", [P, CH, FF], F32R) for n in ("hi", "lo")]
        w2 = [sb(f"w2_{n}", [P, J, DM], F32R) for n in ("hi", "lo")]
        raw1, raw2 = sb("raw1", [P, 2, CH, P]), sb("raw2", [P, 2, DM])
        b1_c, g2_c, be_c, b2_bc = sb("b1_c", [P, J]), sb("g2_c", [P, CH]), sb("be_c", [P, CH]), sb("b2_bc", [P, DM])
        r = sb("r", [P, 2, NB, DM])
        st, part, mean, ve, rstd, expo = (sb("st2", [P, NB, 6]), sb("part2", [P, 4, NB]), sb("mean2", [P, NB]), sb("ve2", [P, NB]),
                                  sb("rstd2", [P, NB]), sb("expo2", [P, NB]))
        hn = sb("hn", [P, 2, DM])
        hTf = sb("hTf", [P, CH, ROWS])
        hT = [sb(f"hT_{n}", [P, CH, ROWS], F32R) for n in ("hi", "lo")]
        gf = sb("gf", [P, 2, ROWS])
        gT = [sb(f"gT_{n}", [P, 2, ROWS], F32R) for n in ("hi", "lo")]
        psH = [ctx.enter_context(nc.psum_tensor(f"psH{i}", [P, ROWS], F32)) for i in range(2)]
        psY = [ctx.enter_context(nc.psum_tensor(f"psY{i}", [P, DM], F32)) for i in range(NB)]
        psX = [ctx.enter_context(nc.psum_tensor(f"psX2{i}", [P, CH, P], F32)) for i in range(2)]
        cols_in, rows_in, r_in, y_out = sem("cols_in"), sem("rows_in"), [sem(f"r_in{i}") for i in range(2)], [sem(f"y_out{i}") for i in range(2)]
        w_in = [sem(f"raw_in{i}") for i in range(2)]
        w_hi, w_ready = sem("w_hi"), sem("w_ready")
        expo_ok, bn_done, part_done, var_ready, rstd_ready, hn_ready, b2_added = (
            sem("expo_ok2"), sem("bn_done2"), sem("part_done2"), sem("var_ready2"), sem("rstd_ready2"), sem("hn_ready"), sem("b2_added"))
        xt_done, xt_copied, h_hi, h_split = sem("xt_done2"), sem("xt_copied2"), sem("h_hi"), sem("h_split")
        up_done, gelu_done, g_hi, g_split, down_done, y_ready = (
            sem("up_done"), sem("gelu_done"), sem("g_hi"), sem("g_split"), sem("down_done"), sem("y_ready"))
        block = ctx.enter_context(nc.Block())
        r_rows = resid.rearrange("b s n -> s b n")
        y_rows = out.rearrange("b s n -> s b n")
        w1_rows = d["W1"].rearrange("(c p) f -> p c f", p=P)
        w2_rows = d["W2"].rearrange("(j p) n -> p j n", p=P)
        NORM_AT = (6, 8, 10, 12)

        def run(eng, group):
            group(0, 0, True, True)
            with eng.Fori(0, (GROUPS - 2) // 2) as i:
                for u in range(2):
                    group(i * 2 + (1 + u), (1 + u) % 2, False, True)
            group(GROUPS - 1, (GROUPS - 1) % 2, False, False)

        def done_before(n, u):
            return (n - u) // 2

        @block.sync
        def _(sp):
            def load_r(n, u):
                at_least(sp, y_out[u], done_before(n, u) * (NB * DMA))
                sp.dma_start(r[:, u, :, :], r_rows[:, bass.ds(n * NB, NB), :]).then_inc(r_in[u], DMA)

            def group(n, u, first, more):
                if more:
                    load_r(n + 1, 1 - u)
                if first:
                    for j in range(J):
                        if j >= 2:
                            sp.wait_ge(w_ready, j - 1)
                        sp.dma_start(raw1[:, j % 2, :, :], w1_rows[:, :, j * P:(j + 1) * P]).then_inc(w_in[j % 2], DMA)
                        sp.dma_start(raw2[:, j % 2, :], w2_rows[:, j, :]).then_inc(w_in[j % 2], DMA)
                for b in range(NB):
                    at_least(sp, y_ready, n * NB + (b + 1))
                    sp.dma_start(y_rows[:, bass.ds(n * NB + b, 1), :], r[:, u, b, :]).then_inc(y_out[u], DMA)

            load_r(0, 0)
            with nc.allow_non_contiguous_dma(reason="columns of biases and gains"):
                sp.dma_start(g2_c[:, :], d["g2"].rearrange("(c p) -> p c", p=P)).then_inc(cols_in, DMA)
                sp.dma_start(be_c[:, :], d["beta2"].rearrange("(c p) -> p c", p=P)).then_inc(cols_in, DMA)
                sp.dma_start(b1_c[:, :], d["b1"].rearrange("(c p) -> p c", p=P)).then_inc(cols_in, DMA)
            sp.dma_start(b2_bc[:, :], d["b2"].rearrange("(a f) -> a f", a=1).to_broadcast([P, DM])).then_inc(rows_in, DMA)
            run(sp, group)
            for i in range(2):
                sp.wait_ge(y_out[i], GROUPS // 2 * NB * DMA)

        @block.gpsimd
        def _(pool):
            def prepare(n, u):
                at_least(pool, var_ready, n + 1)
                pool.tensor_tensor(rstd[:, :], ve[:, :], expo[:, :], ALU.pow).then_inc(rstd_ready, 1)
                for b in range(NB):
                    at_least(pool, hn_ready, n * NB + (b + 1))
                    pool.tensor_tensor(r[:, u, b, :], r[:, u, b, :], b2_bc[:, :], ALU.add).then_inc(b2_added, 1)

            def group(n, u, first, more):
                if more:
                    prepare(n + 1, 1 - u)

            pool.memset(expo[:, :], -0.5).then_inc(expo_ok, 1)
            pool.wait_ge(expo_ok, 1)
            pool.wait_ge(rows_in, DMA)
            prepare(0, 0)
            run(pool, group)

        @block.scalar
        def _(act):
            def copy_hT(n, b):
                at_least(act, xt_done, n * NB + (b + 1))
                if b == 0:
                    at_least(act, h_split, n * CH)
                for c in range(CH):
                    last = act.activation(hTf[:, c, b * P:(b + 1) * P], psX[b % 2][:, c, :], ACT.Identity,
                                          scale=g2_c[:, c:c + 1], bias=be_c[:, c:c + 1])
                last.then_inc(xt_copied, 1)

            def gelu(n, j):
                at_least(act, up_done, n * J + (j + 1))
                at_least(act, g_split, n * J + (j - 1))
                act.activation(gf[:, j % 2, :], psH[j % 2][:, :], ACT.Gelu_apprx_sigmoid,
                               bias=b1_c[:, j:j + 1]).then_inc(gelu_done, 1)

            def split_raw(j):
                act.wait_ge(w_in[j % 2], 2 * DMA * (j // 2 + 1))
                act.activation(w1[0][:, :, j * P:(j + 1) * P], raw1[:, j % 2, :, :], ACT.Copy).then_inc(w_hi, 1)
                act.activation(w2[0][:, j, :], raw2[:, j % 2, :], ACT.Copy).then_inc(w_hi, 1)

            def group(n, u, first, more):
                for j in range(J):
                    if first and j + 2 < J:
                        split_raw(j + 2)
                    gelu(n, j)
                    if more and j in NORM_AT:
                        copy_hT(n + 1, NORM_AT.index(j))

            act.wait_ge(cols_in, 3 * DMA)
            split_raw(0)
            split_raw(1)
            for b in range(NB):
                copy_hT(0, b)
            run(act, group)

        @block.vector
        def _(dve):
            def statistics(n, u, k):
                at_least(dve, r_in[u], (done_before(n, u) + 1) * DMA)
                dve.bn_stats(st[:, k, :], r[:, u, k, :]).then_inc(bn_done, 1)

            def spread(n):
                at_least(dve, hn_ready, n * NB)
                at_least(dve, rstd_ready, n)
                variance(dve, st, part, mean[:, :], ve[:, :], (bn_done, n * NB + NB), part_done, var_ready, n, DM)

            def norm(n, u, b):
                at_least(dve, rstd_ready, n + 1)
                at_least(dve, xt_done, n * NB + (b - 1))
                dve.tensor_scalar(hn[:, b % 2, :], r[:, u, b, :], mean[:, b:b + 1], rstd[:, b:b + 1],
                                  ALU.subtract, ALU.mult).then_inc(hn_ready, 1)

            def split_h(n):
                at_least(dve, xt_copied, n * NB + NB)
                at_least(dve, up_done, n * J)
                for c in range(CH + 1):
                    if c < CH:
                        dve.tensor_copy(hT[0][:, c, :], hTf[:, c, :]).then_inc(h_hi, 1)
                    if c:
                        at_least(dve, h_hi, n * CH + c)
                        dve.tensor_tensor(hT[1][:, c - 1, :], hTf[:, c - 1, :], hT[0][:, c - 1, :].bitcast(F32),
                                          ALU.subtract).then_inc(h_split, 1)

            def split_g(n, j):
                at_least(dve, gelu_done, n * J + (j + 1))
                at_least(dve, down_done, n * J + (j - 1))
                dve.tensor_copy(gT[0][:, j % 2, :], gf[:, j % 2, :]).then_inc(g_hi, 1)
                at_least(dve, g_hi, n * J + (j + 1))
                dve.tensor_tensor(gT[1][:, j % 2, :], gf[:, j % 2, :], gT[0][:, j % 2, :].bitcast(F32),
                                  ALU.subtract).then_inc(g_split, 1)

            def split_raw(j):
                dve.wait_ge(w_hi, 2 * j + 2)
                dve.tensor_tensor(w1[1][:, :, j * P:(j + 1) * P], raw1[:, j % 2, :, :],
                                  w1[0][:, :, j * P:(j + 1) * P].bitcast(F32), ALU.subtract)
                dve.tensor_tensor(w2[1][:, j, :], raw2[:, j % 2, :], w2[0][:, j, :].bitcast(F32),
                                  ALU.subtract).then_inc(w_ready, 1)

            def finish(n, u):
                at_least(dve, down_done, n * J + J)
                at_least(dve, b2_added, n * NB + NB)
                for b in range(NB):
                    dve.tensor_tensor(r[:, u, b, :], psY[b][:, :], r[:, u, b, :], ALU.add).then_inc(y_ready, 1)

            def group(n, u, first, more):
                for j in range(J):
                    if first and j + 2 < J:
                        split_raw(j + 2)
                    split_g(n, j)
                    if more and 1 <= j <= NB:
                        statistics(n + 1, 1 - u, j - 1)
                    if more and j == NB:
                        spread(n + 1)
                    if more and j + 1 in NORM_AT:
                        norm(n + 1, 1 - u, NORM_AT.index(j + 1))
                if more:
                    split_h(n + 1)
                finish(n, u)

            for k in range(NB):
                statistics(0, 0, k)
            spread(0)
            split_raw(0)
            split_raw(1)
            for b in range(NB):
                norm(0, 0, b)
            split_h(0)
            run(dve, group)

        @block.tensor
        def _(pe):
            def three(out_ap, stat, moving, start, stop):
                (sh, sl), (mh, ml) = stat, moving
                pe.matmul(out_ap, sh, mh, start=start, stop=False)
                pe.matmul(out_ap, sh, ml, start=False, stop=False)
                return pe.matmul(out_ap, sl, mh, start=False, stop=stop)

            def transpose_h(n, b):
                at_least(pe, hn_ready, n * NB + (b + 1))
                at_least(pe, xt_copied, n * NB + (b - 1))
                for c in range(CH):
                    last = pe.transpose(psX[b % 2][:, c, :], hn[:, b % 2, c * P:(c + 1) * P], ident[:, :])
                last.then_inc(xt_done, 1)

            def up(n, j, first):
                if first:
                    pe.wait_ge(w_ready, j + 1)
                at_least(pe, gelu_done, n * J + (j - 1))
                for c in range(CH):
                    if j == 0:
                        at_least(pe, h_split, n * CH + (c + 1))
                    last = three(psH[j % 2][:, :], [m[:, c, j * P:(j + 1) * P] for m in w1],
                                 [x[:, c, :] for x in hT], c == 0, c == CH - 1)
                last.then_inc(up_done, 1)

            def down(n, j):
                at_least(pe, g_split, n * J + (j + 1))
                for b in range(NB):
                    if j == 0:
                        at_least(pe, y_ready, (n - 1) * NB + (b + 1))
                    last = three(psY[b][:, :], [x[:, j % 2, b * P:(b + 1) * P] for x in gT],
                                 [m[:, j, :] for m in w2], j == 0, j == J - 1)
                last.then_inc(down_done, 1)

            def group(n, u, first, more):
                for j in range(J):
                    up(n, j, first)
                    if more and j in NORM_AT:
                        transpose_h(n + 1, NORM_AT.index(j))
                    if j:
                        down(n, j - 1)
                down(n, J - 1)

            for b in range(NB):
                transpose_h(0, b)
            run(pe, group)


def layer(nc, d, out):
    B, S, DM = d["x"].shape
    CH, H = DM // P, d["bias"].shape[1]
    assert S == P and DM == 4 * P and H == 16 and B % 4 == 0
    resid = nc.dram_tensor("resid", [B, S, DM], F32, kind="Internal").ap()
    ada_rows = nc.dram_tensor("ada_rows", [B, 2 * DM], F32, kind="Internal").ap()
    with ExitStack() as whole:
        ident = whole.enter_context(nc.sbuf_tensor("ident", [P, P], F32))
        with ExitStack() as ctx:
            sb = lambda name, shape, dt=F32: ctx.enter_context(nc.sbuf_tensor(name, shape, dt))
            w = [[sb(f"w{n}_{part}", [P, CH, DM], F32R) for part in ("hi", "lo")] for n in "qkvo"]
            adaT = sb("adaT", [P, 2 * CH, B])
            bq_s, bk_c, bv_bc = sb("bq_s", [P, CH]), sb("bk_c", [P, CH]), sb("bv_bc", [P, DM])
            kbd = [sb(f"kbd{b}", [P, 2, H // 4, 4, P], F32R) for b in range(2)]
            setup_block(nc, d, w, adaT, ada_rows, ident, bq_s, bk_c, bv_bc, kbd)
            attention_block(nc, d, w, adaT, ada_rows, resid, ident, bq_s, bk_c, bv_bc, kbd)
        feed_block(nc, d, resid, ident, out)


_INS = {"x": "x", "t": "itok_B_34_63", "bias": "fside_Bx16xSxS_0", "mask": "mask_Bx1xSxS_bk0"} | {
    n: f"L0_cond_{n}" for n in ("W_ada", "b_ada", "Wq", "bq", "Wk", "bk", "Wv", "bv", "Wo", "bo",
                                "W1", "b1", "W2", "b2", "g2", "beta2")}


def kernel(**inputs):
    import concourse.bacc as bacc
    from concourse.bass_utils import run_bass_kernel_spmd

    nc = bacc.Bacc("TRN2", target_bir_lowering=False, num_devices=1)
    arrays, d = {}, {}
    for short, name in _INS.items():
        a = np.ascontiguousarray(inputs[name])
        arrays[f"in_{short}"] = a
    half = arrays["in_x"].shape[2] // 2
    arrays["in_freqs"] = np.exp(np.arange(half, dtype=np.float32) * np.float32(-math.log(10000.0) / (half - 1)))
    for name, a in arrays.items():
        d[name[3:]] = nc.dram_tensor(name, a.shape, mybir.dt.from_np(a.dtype), kind="ExternalInput").ap()
    out = nc.dram_tensor("out", arrays["in_x"].shape, F32, kind="ExternalOutput").ap()
    layer(nc, d, out)
    r = run_bass_kernel_spmd(nc, [arrays], core_ids=[0])
    return r.results[0]["out"]
```

```python
import math
from collections import namedtuple
from contextlib import ExitStack

import numpy as np

import concourse.bass as bass
from concourse import mybir

F32 = mybir.dt.float32
F32R = mybir.dt.float32r
I32 = mybir.dt.int32
U8 = mybir.dt.uint8
ACT = mybir.ActivationFunctionType
ALU = mybir.AluOpType

P = 128
EPS = 1e-5
NUM_STEPS, RESCALE = 100.0, 4000.0
LOWEST = -3.0e38
ROUND = 1.5 * 2.0**23
TWO_PI = 2.0 * math.pi
PI_A = 6.28125
PI_B = float(np.float32(np.round((TWO_PI - PI_A) * 2**20) / 2**20))
PI_C = TWO_PI - PI_A - PI_B
DMA = 16


def at_least(eng, sem, count):
    if isinstance(count, int) and count <= 0:
        return
    eng.wait_ge(sem, count)


def variance(dve, st, part, mean, ve, stats_ok, done, var_ready, n, rows):
    even, odd, half = st[:, :, 0:3], st[:, :, 3:6], rows // 2
    at_least(dve, *stats_ok)
    dve.tensor_tensor(part[:, 0, :], even[:, :, 1], odd[:, :, 1], ALU.subtract)
    dve.tensor_tensor(part[:, 1, :], even[:, :, 2], odd[:, :, 2], ALU.add)
    dve.tensor_tensor(part[:, 2, :], even[:, :, 1], odd[:, :, 1], ALU.add).then_inc(done, 1)
    at_least(dve, done, n * 3 + 1)
    dve.tensor_tensor(part[:, 3, :], part[:, 0, :], part[:, 0, :], ALU.mult)
    dve.tensor_scalar(mean, part[:, 2, :], 0.5, None, ALU.mult).then_inc(done, 1)
    at_least(dve, done, n * 3 + 2)
    dve.scalar_tensor_tensor(out=part[:, 0, :], in0=part[:, 3, :], scalar=half / 2.0, in1=part[:, 1, :],
                             op0=ALU.mult, op1=ALU.add).then_inc(done, 1)
    at_least(dve, done, n * 3 + 3)
    dve.tensor_scalar(ve, part[:, 0, :], 1.0 / rows, EPS, ALU.mult, ALU.add).then_inc(var_ready, 1)


def split(dve, hi, lo, of, hi_sem, done, n):
    dve.tensor_copy(hi, of).then_inc(hi_sem, 1)
    at_least(dve, hi_sem, n + 1)
    dve.tensor_tensor(lo, of, hi.bitcast(F32), ALU.subtract).then_inc(done, 1)


class FirstNorm:

    def __init__(self, nc, ctx, x, ident, psX):
        sb = lambda name, shape, dt=F32: ctx.enter_context(nc.sbuf_tensor(name, shape, dt))
        sem = lambda name: ctx.enter_context(nc.semaphore(name))
        B, _, DM = x.shape
        self.DM, self.CH, self.ident, self.psX = DM, DM // P, ident, psX
        self.rows = x.rearrange("b s n -> s b n")
        self.xin, self.xn = sb("xin", [P, 2, DM]), sb("xn", [P, 2, DM])
        self.st, self.part = sb("st", [P, 2, 6]), sb("part", [P, 4, 2])
        self.mean, self.ve, self.rstd, self.expo = sb("mean", [P, 2]), sb("ve", [P, 2]), sb("rstd", [P, 2]), sb("expo", [P, 2])
        self.adaT = sb("adaT", [P, 2 * self.CH, B])
        self.xTf = sb("xTf", [P, self.CH, P])
        self.xT = [sb(f"xT_{n}", [P, self.CH, 2 * P], F32R) for n in ("hi", "lo")]
        self.x_in, self.bn_done, self.part_done, self.var_ready, self.rstd_ready, self.xn_ready = (
            sem("x_in"), sem("bn_done"), sem("part_done"), sem("var_ready"), sem("rstd_ready"), sem("xn_ready"))
        self.xt_done, self.xt_copied, self.x_hi, self.x_split = sem("xt_done"), sem("xt_copied"), sem("x_hi"), sem("x_split")
        self.res_ready, self.q_done = sem("res_ready"), sem("q_done")

    def load(self, sp, q):
        at_least(sp, self.xn_ready, q * 2)
        sp.dma_start(self.xin[:, :, :], self.rows[:, bass.ds(q * 2, 2), :]).then_inc(self.x_in, DMA)

    def statistics(self, dve, q):
        at_least(dve, self.x_in, (q + 1) * DMA)
        at_least(dve, self.xn_ready, q * 2)
        for b in range(2):
            dve.bn_stats(self.st[:, b, :], self.xin[:, b, :]).then_inc(self.bn_done, 1)
        at_least(dve, self.rstd_ready, q)
        variance(dve, self.st, self.part, self.mean[:, :], self.ve[:, :], (self.bn_done, q * 2 + 2),
                 self.part_done, self.var_ready, q, self.DM)

    def root(self, pool, q):
        at_least(pool, self.var_ready, q + 1)
        pool.tensor_tensor(self.rstd[:, :], self.ve[:, :], self.expo[:, :], ALU.pow).then_inc(self.rstd_ready, 1)

    def normalize(self, dve, q, b):
        at_least(dve, self.rstd_ready, q + 1)
        at_least(dve, self.xt_done, q * 2)
        at_least(dve, self.res_ready, q * 2)
        dve.tensor_scalar(self.xn[:, b, :], self.xin[:, b, :], self.mean[:, b:b + 1], self.rstd[:, b:b + 1],
                          ALU.subtract, ALU.mult).then_inc(self.xn_ready, 1)

    def transpose(self, pe, q, b):
        at_least(pe, self.xn_ready, q * 2 + (b + 1))
        at_least(pe, self.xt_copied, q * 2 + b)
        for c in range(self.CH):
            last = pe.transpose(self.psX[:, c, :], self.xn[:, b, c * P:(c + 1) * P], self.ident[:, :])
        last.then_inc(self.xt_done, 1)

    def copy(self, act, q, b):
        at_least(act, self.xt_done, q * 2 + (b + 1))
        at_least(act, self.x_split, q * 2 + b)
        at = bass.ds(q * 2 + b, 1)
        for c in range(self.CH):
            last = act.activation(self.xTf[:, c, :], self.psX[:, c, :], ACT.Identity,
                                  scale=self.adaT[:, c, at], bias=self.adaT[:, self.CH + c, at])
        last.then_inc(self.xt_copied, 1)

    def split(self, dve, q, b):
        at_least(dve, self.xt_copied, q * 2 + (b + 1))
        at_least(dve, self.q_done, q * 4)
        at = slice(b * P, (b + 1) * P)
        split(dve, self.xT[0][:, :, at], self.xT[1][:, :, at], self.xTf[:, :, :], self.x_hi, self.x_split, q * 2 + b)


class SecondNorm:

    def __init__(self, nc, ctx, resid, ident, psX, NB):
        sb = lambda name, shape, dt=F32: ctx.enter_context(nc.sbuf_tensor(name, shape, dt))
        sem = lambda name: ctx.enter_context(nc.semaphore(name))
        DM = resid.shape[2]
        self.DM, self.CH, self.NB, self.ident, self.psX = DM, DM // P, NB, ident, psX
        self.rows = resid.rearrange("b s n -> s b n")
        self.hTf = sb("hTf", [P, self.CH, NB * P])
        self.hn, self.gf = sb("hn", [P, 2, DM]), sb("gf", [P, 2, NB * P])
        self.hT = [sb(f"hT_{n}", [P, self.CH, NB * P], F32R) for n in ("hi", "lo")]
        self.r = [sb(f"r{u}", [P, NB, DM]) for u in range(2)]
        self.st, self.part, self.mean, self.ve = sb("st2", [P, NB, 6]), sb("part2", [P, 4, NB]), sb("mean2", [P, NB]), sb("ve2", [P, NB])
        self.rstd, self.expo, self.g2_c, self.be_c = sb("rstd2", [P, NB]), sb("expo2", [P, NB]), sb("g2_c", [P, self.CH]), sb("be_c", [P, self.CH])
        self.r_in, self.y_out = [sem(f"r_in{i}") for i in range(2)], [sem(f"y_out{i}") for i in range(2)]
        self.cols_in, self.expo_ok, self.bn_done, self.part_done, self.var_ready, self.rstd_ready, self.hn_ready = (
            sem("cols_in"), sem("expo_ok2"), sem("bn_done2"), sem("part_done2"), sem("var_ready2"), sem("rstd_ready2"), sem("hn_ready"))
        self.xt_done, self.xt_copied, self.h_hi, self.h_split = sem("xt_done2"), sem("xt_copied2"), sem("h_hi"), sem("h_split")
        self.up_done = sem("up_done")

    def load(self, sp, n, u):
        at_least(sp, self.y_out[u], (n - u) // 2 * (self.NB * DMA))
        sp.dma_start(self.r[u][:, :, :], self.rows[:, bass.ds(n * self.NB, self.NB), :]).then_inc(self.r_in[u], DMA)

    def statistics(self, dve, n, u, b):
        at_least(dve, self.r_in[u], ((n - u) // 2 + 1) * DMA)
        dve.bn_stats(self.st[:, b, :], self.r[u][:, b, :]).then_inc(self.bn_done, 1)

    def spread(self, dve, n):
        at_least(dve, self.hn_ready, n * self.NB)
        at_least(dve, self.rstd_ready, n)
        variance(dve, self.st, self.part, self.mean[:, :], self.ve[:, :], (self.bn_done, n * self.NB + self.NB),
                 self.part_done, self.var_ready, n, self.DM)

    def root(self, pool, n):
        at_least(pool, self.var_ready, n + 1)
        pool.tensor_tensor(self.rstd[:, :], self.ve[:, :], self.expo[:, :], ALU.pow).then_inc(self.rstd_ready, 1)

    def normalize(self, dve, n, u, b):
        at_least(dve, self.rstd_ready, n + 1)
        at_least(dve, self.xt_done, n * self.NB + (b - 1))
        dve.tensor_scalar(self.hn[:, b % 2, :], self.r[u][:, b, :], self.mean[:, b:b + 1], self.rstd[:, b:b + 1],
                          ALU.subtract, ALU.mult).then_inc(self.hn_ready, 1)

    def transpose(self, pe, n, b):
        at_least(pe, self.hn_ready, n * self.NB + (b + 1))
        at_least(pe, self.xt_copied, n * self.NB + (b - 1))
        for c in range(self.CH):
            last = pe.transpose(self.psX[b % 2][:, c, :], self.hn[:, b % 2, c * P:(c + 1) * P], self.ident[:, :])
        last.then_inc(self.xt_done, 1)

    def copy(self, act, n, b):
        at_least(act, self.xt_done, n * self.NB + (b + 1))
        if b == 0:
            at_least(act, self.h_split, n * self.CH)
        for c in range(self.CH):
            last = act.activation(self.hTf[:, c, b * P:(b + 1) * P], self.psX[b % 2][:, c, :], ACT.Identity,
                                  scale=self.g2_c[:, c:c + 1], bias=self.be_c[:, c:c + 1])
        last.then_inc(self.xt_copied, 1)

    def split(self, dve, n):
        at_least(dve, self.xt_copied, n * self.NB + self.NB)
        at_least(dve, self.up_done, n * 16)
        for c in range(self.CH + 1):
            if c < self.CH:
                dve.tensor_copy(self.hT[0][:, c, :], self.hTf[:, c, :]).then_inc(self.h_hi, 1)
            if c:
                at_least(dve, self.h_hi, n * self.CH + c)
                dve.tensor_tensor(self.hT[1][:, c - 1, :], self.hTf[:, c - 1, :], self.hT[0][:, c - 1, :].bitcast(F32),
                                  ALU.subtract).then_inc(self.h_split, 1)


class RawWeights:

    def __init__(self, nc, ctx, d, raw_o):
        self.raw1 = raw_o[:, 0:2, :].rearrange("p u (c k) -> p u c k", k=P)
        self.raw2 = raw_o[:, 2:4, :]
        self.rows1 = d["W1"].rearrange("(c p) f -> p c f", p=P)
        self.rows2 = d["W2"].rearrange("(j p) n -> p j n", p=P)
        self.arrived = [ctx.enter_context(nc.semaphore(f"raw_in{i}")) for i in range(2)]

    def load(self, sp, j):
        sp.dma_start(self.raw1[:, j % 2, :, :], self.rows1[:, :, j * P:(j + 1) * P]).then_inc(self.arrived[j % 2], DMA)
        sp.dma_start(self.raw2[:, j % 2, :], self.rows2[:, j, :]).then_inc(self.arrived[j % 2], DMA)


def setup_block(nc, d, w, norm, ada_rows, bq_s, bk_c, bv_bc, kbd, raw_o, wo_in):
    B, DM = d["x"].shape[0], d["x"].shape[2]
    HALF, CH, HD = DM // 2, DM // P, DM // 16
    assert 2 * B == P
    ident = norm.ident
    with ExitStack() as ctx:
        sb = lambda name, shape, dt=F32: ctx.enter_context(nc.sbuf_tensor(name, shape, dt))
        sem = lambda name: ctx.enter_context(nc.semaphore(name))
        names = "vkq"
        raw = [sb(f"raw_{n}", [P, CH, DM]) for n in names]
        split_w = [w["qkvo".index(n)] for n in names]
        w_ada = sb("w_ada", [P, CH, 2 * DM])
        b_ada = sb("b_ada", [B, 2 * DM])
        bo_bc = sb("bo_bc", [B, DM])
        bq_raw = sb("bq_raw", [P, CH])
        t_int = sb("t_int", [P, 1], I32)
        col = sb("col", [P, 8])
        quarter = sb("quarter", [P, 2])
        q_hi = sb("q_hi", [P, 1], F32R)
        freqs, angle, turns, rest = (sb(n, [P, HALF]) for n in ("freqs", "angle", "turns", "rest"))
        emb, expm, gate = (sb(n, [P, HALF]) for n in ("emb", "expm", "gate"))
        embT = sb("embT", [P, 2, CH // 2, B])
        ada = sb("ada", [B, 2 * DM])
        rows = sb("rows", [B, 2 * DM])
        psT = ctx.enter_context(nc.psum_tensor("psT", [P, CH // 2, 2 * B], F32))
        psA = ctx.enter_context(nc.psum_tensor("psA", [B, 2, DM], F32))
        psC = ctx.enter_context(nc.psum_tensor("psC_ada", [P, 2 * CH, B], F32))
        small_in, ada_in, bias_in, w_in = sem("small_in"), sem("ada_in"), sem("row_bias_in"), [sem(f"w_in{i}") for i in range(3)]
        zeroed, ident_ok, gate_ok, sin_ok, exp_ok = sem("zeroed"), sem("ident_ok"), sem("gate_ok"), sem("sin_ok"), sem("exp_ok")
        quarter_ok, rest_ok, chain, gate_turned, embT_ok, ada_done, ada_ok, ada_turned, adaT_ok, rows_ok, rows_out, w_hi = (
            sem("quarter_ok"), sem("rest_ok"), sem("chain"), sem("gate_turned"), sem("embT_ok"), sem("ada_done"),
            sem("ada_ok"), sem("ada_turned"), sem("adaT_ok"), sem("rows_ok"), sem("rows_out"), sem("w_hi"))
        block = ctx.enter_context(nc.Block())

        def low(eng, i, chunks):
            eng.wait_ge(w_hi, i + 1)
            eng.tensor_tensor(split_w[i][1][:, chunks, :], raw[i][:, chunks, :],
                              split_w[i][0][:, chunks, :].bitcast(F32), ALU.subtract)

        @block.sync
        def _(sp):
            for half in (slice(0, B), slice(B, 2 * B)):
                sp.dma_start(t_int[half, :], d["t"].rearrange("(b a) -> b a", a=1)).then_inc(small_in, DMA)
            sp.dma_start(freqs[:, :], d["freqs"].rearrange("(a f) -> a f", a=1).to_broadcast([P, HALF])).then_inc(small_in, DMA)
            norm.load(sp, 0)
            sp.dma_start(w_ada[:, :, :], d["W_ada"].rearrange("(c p) n -> p c n", p=P)).then_inc(ada_in, DMA)
            with nc.allow_non_contiguous_dma(reason="bias columns"):
                for t, name in ((bq_raw, "bq"), (bk_c, "bk")):
                    sp.dma_start(t[:, :], d[name].rearrange("(c p) -> p c", p=P)).then_inc(bias_in, DMA)
            for i, n in enumerate(names):
                sp.dma_start(raw[i][:, :, :], d["W" + n].rearrange("(c p) n -> p c n", p=P)).then_inc(w_in[i], DMA)
                if i == 0:
                    sp.dma_start(b_ada[:, :], d["b_ada"].rearrange("(a f) -> a f", a=1).to_broadcast([B, 2 * DM])).then_inc(bias_in, DMA)
                    sp.dma_start(bo_bc[:, :], d["bo"].rearrange("(a f) -> a f", a=1).to_broadcast([B, DM])).then_inc(bias_in, DMA)
                    sp.dma_start(bv_bc[:, :], d["bv"].rearrange("(a f) -> a f", a=1).to_broadcast([P, DM])).then_inc(bias_in, DMA)
            sp.dma_start(raw_o[:, :, :], d["Wo"].rearrange("(c p) n -> p c n", p=P)).then_inc(wo_in, DMA)
            sp.wait_ge(rows_ok, 2)
            sp.dma_start(ada_rows, rows[:, :]).then_inc(rows_out, DMA)
            sp.wait_ge(rows_out, DMA)

        @block.gpsimd
        def _(pool):
            for a in range(2):
                for c, unit in enumerate((1.0, TWO_PI)):
                    pool.memset(quarter[a * B:(a + 1) * B, c:c + 1], 0.25 * unit * a).then_inc(quarter_ok, 1)
            pool.wait_ge(quarter_ok, 4)
            pool.memset(norm.expo[:, :], -0.5).then_inc(quarter_ok, 1)
            pool.memset(ident[:, :], 0.0).then_inc(ident_ok, 1)
            pool.wait_ge(ident_ok, 1)
            pool.affine_select(out=ident[:, :], in_=ident[:, :], compare_op=ALU.not_equal, fill=1.0,
                               base=0, pattern=[[-1, P]], channel_multiplier=1).then_inc(ident_ok, 1)
            pool.wait_ge(quarter_ok, 5)
            norm.root(pool, 0)
            for t in kbd:
                pool.memset(t[:, :, :, :, :].bitcast(F32), 0.0).then_inc(zeroed, 1)
            pool.wait_ge(zeroed, len(kbd))
            low(pool, 2, slice(CH // 2, CH))

        @block.scalar
        def _(act):
            def high(i):
                act.wait_ge(w_in[i], DMA)
                act.activation(split_w[i][0][:, :, :], raw[i][:, :, :], ACT.Copy).then_inc(w_hi, 1)

            act.wait_ge(rest_ok, 1)
            act.activation(emb[:, :], rest[:, :], ACT.Sin).then_inc(sin_ok, 1)
            act.wait_ge(sin_ok, 1)
            act.activation(expm[:, :], emb[:, :], ACT.Exp, scale=-1.0).then_inc(exp_ok, 1)
            for i in range(3):
                high(i)
            act.wait_ge(adaT_ok, 1)
            norm.copy(act, 0, 0)

        @block.tensor
        def _(pe):
            pe.wait_ge(ident_ok, 2)
            pe.wait_ge(gate_ok, 1)
            for c in range(CH // 2):
                last = pe.transpose(psT[:, c, :], gate[:, c * P:(c + 1) * P], ident[:, :])
            last.then_inc(gate_turned, 1)
            norm.transpose(pe, 0, 0)
            pe.wait_ge(embT_ok, 1)
            pe.wait_ge(ada_in, DMA)
            for h in range(2):
                for c in range(CH):
                    last = pe.matmul(psA[:, h, :], embT[:, c // 2, c % 2, :], w_ada[:, c, h * DM:(h + 1) * DM],
                                     start=(c == 0), stop=(c == CH - 1))
                last.then_inc(ada_done, 1)
            for c in range(2 * CH):
                if c % CH == 0:
                    pe.wait_ge(ada_ok, c // CH + 1)
                last = pe.transpose(psC[:, c, :], ada[:, c * P:(c + 1) * P], ident[0:B, 0:B])
            last.then_inc(ada_turned, 1)

        @block.vector
        def _(dve):
            count = [0]

            def then(ins):
                count[0] += 1
                ins.then_inc(chain, 1)
                dve.wait_ge(chain, count[0])

            dve.wait_ge(small_in, 3 * DMA)
            then(dve.tensor_copy(col[:, 0:1], t_int[:, :]))
            then(dve.tensor_scalar(col[:, 1:2], col[:, 0:1], 1.0 / NUM_STEPS, None, ALU.mult))
            then(dve.tensor_copy(q_hi[:, :], col[:, 1:2]))
            then(dve.tensor_tensor(col[:, 2:3], col[:, 1:2], q_hi[:, :].bitcast(F32), ALU.subtract))
            then(dve.scalar_tensor_tensor(out=col[:, 3:4], in0=q_hi[:, :].bitcast(F32), scalar=-NUM_STEPS,
                                          in1=col[:, 0:1], op0=ALU.mult, op1=ALU.add))
            then(dve.scalar_tensor_tensor(out=col[:, 4:5], in0=col[:, 2:3], scalar=-NUM_STEPS,
                                          in1=col[:, 3:4], op0=ALU.mult, op1=ALU.add))
            then(dve.scalar_tensor_tensor(out=col[:, 5:6], in0=col[:, 4:5], scalar=1.0 / NUM_STEPS,
                                          in1=col[:, 1:2], op0=ALU.mult, op1=ALU.add))
            then(dve.tensor_scalar(col[:, 6:7], col[:, 5:6], RESCALE, None, ALU.mult))
            then(dve.tensor_scalar(angle[:, :], freqs[:, :], col[:, 6:7], None, ALU.mult))
            k, r = turns[:, :], rest[:, :]
            dve.wait_ge(quarter_ok, 5)
            then(dve.tensor_scalar(k, angle[:, :], 1.0 / TWO_PI, quarter[:, 0:1], ALU.mult, ALU.add))
            then(dve.tensor_scalar(k, k, ROUND, None, ALU.add))
            then(dve.tensor_scalar(k, k, ROUND, None, ALU.subtract))
            then(dve.scalar_tensor_tensor(out=r, in0=k, scalar=-PI_A, in1=angle[:, :], op0=ALU.mult, op1=ALU.add))
            then(dve.scalar_tensor_tensor(out=r, in0=k, scalar=-PI_B, in1=r, op0=ALU.mult, op1=ALU.add))
            then(dve.scalar_tensor_tensor(out=r, in0=k, scalar=-PI_C, in1=r, op0=ALU.mult, op1=ALU.add))
            then(dve.tensor_scalar(r, r, quarter[:, 1:2], None, ALU.add))
            dve.tensor_scalar(r, r, 3.1415925, -3.1415925, ALU.min, ALU.max).then_inc(rest_ok, 1)
            norm.statistics(dve, 0)
            dve.wait_ge(exp_ok, 1)
            then(dve.tensor_scalar(expm[:, :], expm[:, :], 1.0, None, ALU.add))
            then(dve.reciprocal(expm[:, :], expm[:, :]))
            dve.tensor_tensor(gate[:, :], emb[:, :], expm[:, :], ALU.mult).then_inc(gate_ok, 1)
            for b in range(2):
                norm.normalize(dve, 0, b)
            dve.wait_ge(gate_turned, 1)
            dve.tensor_copy(embT[:, :, :, :], psT[:, :, :].rearrange("p c (a b) -> p a c b", a=2)).then_inc(embT_ok, 1)
            dve.wait_ge(bias_in, 5 * DMA)
            dve.tensor_scalar(bq_s[:, :], bq_raw[:, :], HD ** -0.5, None, ALU.mult)
            low(dve, 0, slice(0, CH))
            dve.wait_ge(ada_done, 1)
            dve.scalar_tensor_tensor(out=ada[:, 0:DM], in0=psA[:, 0, :], scalar=1.0, in1=b_ada[:, 0:DM],
                                     op0=ALU.add, op1=ALU.add).then_inc(ada_ok, 1)
            low(dve, 1, slice(0, CH))
            dve.wait_ge(ada_done, 2)
            dve.tensor_tensor(ada[:, DM:], psA[:, 1, :], b_ada[:, DM:], ALU.add).then_inc(ada_ok, 1)
            dve.wait_ge(ada_turned, 1)
            dve.tensor_copy(norm.adaT[:, :, :], psC[:, :, :]).then_inc(adaT_ok, 1)
            dve.wait_ge(ada_ok, 2)
            dve.tensor_copy(rows[:, 0:DM], ada[:, 0:DM]).then_inc(rows_ok, 1)
            dve.tensor_tensor(rows[:, DM:], ada[:, DM:], bo_bc[:, :], ALU.add).then_inc(rows_ok, 1)
            low(dve, 2, slice(0, CH // 2))
            norm.split(dve, 0, 0)


Stages = namedtuple("Stages", "attn prev proj turn norm start tail")


def stages(p, pairs):
    there = lambda q: 0 <= q < pairs
    return Stages(there(p), there(p - 1), there(p + 1), p >= 0 and there(p + 1), there(p + 2), p == -1, p == pairs - 1)


def attention_block(nc, d, w, norm, ada_rows, resid, psD, bq_s, bk_c, bv_bc, kbd, raw_o, wo_in, second, raws):
    B, S, DM = d["x"].shape
    H = d["bias"].shape[1]
    HD, CH = DM // H, DM // P
    HG = P // HD
    G = H // HG
    PAIRS, SLOTS = B // 2, 2 * G
    wq, wk, wv, wo = w
    with ExitStack() as ctx:
        sb = lambda name, shape, dt=F32: ctx.enter_context(nc.sbuf_tensor(name, shape, dt))
        sem = lambda name: ctx.enter_context(nc.semaphore(name))
        xres = sb("xres", [P, 2, 2, DM])
        adab = sb("adab", [P, 2, 2 * DM])
        kf, qf = sb("kf", [P, 2, 2 * P]), sb("qf", [P, 2, 2 * P])
        qT = [sb(f"qT_{n}", [P, G, 2 * P], F32R) for n in ("hi", "lo")]
        kT = sb("kT", [P, 2, G, 2 * P], F32R)
        v = sb("v", [P, 2, 2, DM])
        bias = sb("bias", [P, 2, H, S])
        mask = sb("mask", [P, 2, S], U8)
        mneg = sb("mneg", [P, 2, S])
        s = sb("s", [P, 2, HG, S])
        mx, nmx = sb("mx", [P, 2, HG]), sb("nmx", [P, 2, HG])
        sums, rinv = sb("sums", [P, 2, HG]), sb("rinv", [P, 2, HG])
        pT = sb("pT", [P, 2, HG, P])
        cT = [sb(f"cT_{n}", [P, G, P], F32R) for n in ("hi", "lo")]
        rout = sb("rout", [P, 2, DM])
        psS = [ctx.enter_context(nc.psum_tensor(f"psS{i}", [P, HG, S], F32)) for i in range(2)]
        psP = [ctx.enter_context(nc.psum_tensor(f"psP{i}", [P, HG, P], F32)) for i in range(2)]
        psC = ctx.enter_context(nc.psum_tensor("psC", [P, G, P], F32))
        adab_in = sem("adab_in")
        bias_in = [sem(f"bias_in{b}") for b in range(2)]
        kbd_in = [sem(f"kbd_in{b}") for b in range(2)]
        r_out = [sem(f"r_out{b}") for b in range(2)]
        res_half, wo_hi, wo_split = sem("res_half"), sem("wo_hi"), sem("wo_split")
        v_done, v_ready = sem("v_done"), sem("v_ready")
        k_done, k_copied, k_hi, k_split = sem("k_done"), sem("k_copied"), sem("k_hi"), sem("k_split")
        q_copied, q_hi, q_split = sem("q_copied"), sem("q_hi"), sem("q_split")
        q_done, res_ready, xT, ident = norm.q_done, norm.res_ready, norm.xT, norm.ident
        mask_in = [sem(f"mask_in{b}") for b in range(2)]
        neg_ready = [sem(f"neg_ready{b}") for b in range(2)]
        bias_ready = [sem(f"bias_ready{b}") for b in range(2)]
        qk_done, score_ready, max_done, nmax_ready, exp_done = sem("qk_done"), sem("score_ready"), sem("max_done"), sem("nmax_ready"), sem("exp_done")
        rinv_ready, prob_ready = sem("rinv_ready"), sem("prob_ready")
        pt_done, pt_copied, pv_done = sem("pt_done"), sem("pt_copied"), sem("pv_done")
        ctx_hi, ctx_split, o_done, r_ready = sem("ctx_hi"), sem("ctx_split"), sem("o_done"), sem("r_ready")
        block = ctx.enter_context(nc.Block())

        bias_rows = d["bias"].rearrange("b h q k -> q b h k")
        mask_rows = d["mask"].rearrange("b a q k -> q b (a k)")
        r_rows = resid.rearrange("b s n -> s b n")

        def run(eng, step):
            first, last = 2, PAIRS - 3
            for p in range(-1, first):
                step(p, p % 2, stages(p, PAIRS))
            with eng.Fori(0, (last - first + 1) // 2) as i:
                for u in range(2):
                    step(i * 2 + (first + u), u, Stages(True, True, True, True, True, False, False))
            for p in range(last + 1, PAIRS + 1):
                step(p, p % 2, stages(p, PAIRS))

        @block.sync
        def _(sp):
            def load_bias(q, b):
                at_least(sp, score_ready, (q - 1) * SLOTS + (G * b + G))
                for half in (slice(0, H // 2), slice(H // 2, H)):
                    sp.dma_start(bias[:, b, half, :], bias_rows[:, bass.ds(q * 2 + b, 1), half, :]).then_inc(bias_in[b], DMA)
                sp.dma_start(mask[:, b, :], mask_rows[:, bass.ds(q * 2 + b, 1), :]).then_inc(mask_in[b], DMA)

            def spread_k(q, b):
                at_least(sp, k_split, q * G + G)
                at_least(sp, qk_done, (q - 1) * SLOTS + (G * b + G))
                for j in range(HG):
                    rows = slice(HD * j, HD * j + HD)
                    sp.dma_start(kbd[b][rows, :, :, j, :].bitcast(F32), kT[rows, :, :, b * P:(b + 1) * P].bitcast(F32)).then_inc(kbd_in[b], DMA)

            def store(q, b):
                at_least(sp, r_ready, q * 2 + (b + 1))
                sp.dma_start(r_rows[:, bass.ds(q * 2 + b, 1), :], rout[:, b, :]).then_inc(r_out[b], DMA)

            def load_first_group():
                sp.wait_ge(v_done, B)
                for b in range(2):
                    sp.wait_ge(r_out[b], second.NB // 2 * DMA)
                second.load(sp, 0, 0)
                for j in range(2):
                    raws.load(sp, j)

            def step(p, u, on):
                if on.start:
                    with nc.allow_non_contiguous_dma(reason="columns of gains and offsets"):
                        for t, name in ((second.g2_c, "g2"), (second.be_c, "beta2")):
                            sp.dma_start(t[:, :], d[name].rearrange("(c p) -> p c", p=P)).then_inc(second.cols_in, DMA)
                if on.attn:
                    load_bias(p, 1)
                    spread_k(p, 1)
                if on.tail:
                    load_first_group()
                if on.norm:
                    norm.load(sp, p + 2)
                if on.proj:
                    at_least(sp, res_ready, p * 2 + 2)
                    sp.dma_start(adab[:, :, :], ada_rows[bass.ds(p * 2 + 2, 2), :].unsqueeze(0)
                                 .to_broadcast([P, 2, 2 * DM])).then_inc(adab_in, DMA)
                if on.prev:
                    store(p - 1, 0)
                if on.proj:
                    load_bias(p + 1, 0)
                    spread_k(p + 1, 0)
                if on.prev:
                    store(p - 1, 1)

            run(sp, step)
            for b in range(2):
                sp.wait_ge(r_out[b], DMA * PAIRS)

        @block.gpsimd
        def _(pool):
            def add_mask(q, b, g):
                at_least(pool, bias_in[b], (q + 1) * (2 * DMA))
                at_least(pool, neg_ready[b], q + 1)
                heads = slice(HG * g, HG * g + HG)
                pool.tensor_tensor(bias[:, b, heads, :], bias[:, b, heads, :],
                                   mneg[:, b, :].unsqueeze(1).to_broadcast([P, HG, S]), ALU.add).then_inc(bias_ready[b], 1)

            def normalize_p(t, i):
                at_least(pool, rinv_ready, t + 1)
                pool.tensor_tensor(s[:, i, :, :], s[:, i, :, :], rinv[:, i, :].unsqueeze(2).to_broadcast([P, HG, S]),
                                   ALU.mult).then_inc(prob_ready, 1)

            def residual(q, u, b, prev):
                at_least(pool, norm.xn_ready, q * 2 + (b + 1))
                at_least(pool, adab_in, (q + 1) * DMA)
                if prev:
                    at_least(pool, r_ready, (q - 2) * 2 + (b + 1))
                pool.tensor_tensor(xres[:, u, b, :], norm.xn[:, b, :], adab[:, b, 0:DM], ALU.mult).then_inc(res_half, 1)
                at_least(pool, res_half, q * 2 + (b + 1))
                pool.tensor_tensor(xres[:, u, b, :], xres[:, u, b, :], adab[:, b, DM:], ALU.add).then_inc(res_ready, 1)

            def step(p, u, on):
                for n in range(SLOTS):
                    b, g = n // G, n % G
                    if on.attn and n or on.prev and n == 0:
                        normalize_p(p * SLOTS + n - 1, (g - 1) % 2)
                    if g == 0 and on.attn:
                        add_mask(p, b, G - 1)
                    if g and b == 0 and on.attn:
                        add_mask(p, 1, g - 1)
                    if g and b == 1 and on.proj:
                        add_mask(p + 1, 0, g - 1)
                    if n in (3, 5) and on.proj:
                        residual(p + 1, 1 - u, n // 4, on.prev)
                    if n == 6 and on.norm:
                        norm.root(pool, p + 2)
                    if n == 4 and on.tail:
                        second.root(pool, 0)

            pool.memset(second.expo[:, :], -0.5).then_inc(second.expo_ok, 1)
            pool.wait_ge(second.expo_ok, 1)
            run(pool, step)

        @block.scalar
        def _(act):
            def copy_k(q, g):
                at_least(act, k_done, q * G + (g + 1))
                at_least(act, k_split, q * G + (g - 1))
                act.activation(kf[:, g % 2, :], psD[g % 2][:, 0:2 * P], ACT.Identity,
                               bias=bk_c[:, g:g + 1]).then_inc(k_copied, 1)

            def copy_q(q, g):
                at_least(act, q_done, q * G + (g + 1))
                at_least(act, q_split, q * G + (g - 1))
                act.activation(qf[:, g % 2, :], psD[(g + 1) % 2 if g < 2 else 1][:, 0:2 * P], ACT.Identity,
                               bias=bq_s[:, g:g + 1], scale=HD ** -0.5).then_inc(q_copied, 1)

            def copy_pT(t, i):
                at_least(act, pt_done, t + 1)
                at_least(act, pv_done, t - 1)
                act.activation(pT[:, i, :, :], psP[i][:, :, :], ACT.Copy).then_inc(pt_copied, 1)

            def exps(t, g):
                at_least(act, nmax_ready, t + 1)
                for j in range(HG):
                    last = act.activation(s[:, g % 2, j, :], s[:, g % 2, j, :], ACT.Exp,
                                          bias=nmx[:, g % 2, j:j + 1], accum_out=sums[:, g % 2, j:j + 1])
                last.then_inc(exp_done, 1)

            def step(p, u, on):
                for n in range(SLOTS):
                    b, g = n // G, n % G
                    t = p * SLOTS + n
                    if n < 2 and on.prev or n >= 2 and on.attn:
                        copy_pT(t - 2, g % 2)
                    if on.turn and n < 2 or on.start and n == 1:
                        norm.copy(act, p + 1, n)
                    if on.start and n == 4:
                        act.wait_ge(wo_in, DMA)
                        act.activation(wo[0][:, :, :], raw_o[:, :, :], ACT.Copy).then_inc(wo_hi, 1)
                    if on.proj and n in (2, 3):
                        copy_k(p + 1, 2 * n - 4)
                    if on.proj and n in (5, 6):
                        copy_q(p + 1, 2 * n - 10)
                    if on.attn:
                        exps(t, g)
                    if on.proj and n in (2, 3):
                        copy_k(p + 1, 2 * n - 3)
                    if on.proj and n in (5, 7):
                        copy_q(p + 1, n - 4)
                    if on.tail and n == 5:
                        act.wait_ge(q_done, PAIRS * G)
                        act.wait_ge(second.cols_in, 2 * DMA)
                    if on.tail and n >= 5:
                        second.copy(act, 0, n - 5)
                    if n == 0 and not on.attn and on.prev:
                        second.copy(act, 0, 3)

            run(act, step)

        @block.vector
        def _(dve):
            def split_k(q, g):
                at_least(dve, k_copied, q * G + (g + 1))
                at_least(dve, kbd_in[1], q * (HG * DMA))
                split(dve, kT[:, 0, g, :], kT[:, 1, g, :], kf[:, g % 2, :], k_hi, k_split, q * G + g)

            def split_q(q, g):
                at_least(dve, q_copied, q * G + (g + 1))
                at_least(dve, qk_done, (q - 1) * SLOTS + (G + g + 1))
                split(dve, qT[0][:, g, :], qT[1][:, g, :], qf[:, g % 2, :], q_hi, q_split, q * G + g)

            def add_bv(q, u, b):
                at_least(dve, v_done, q * 2 + (b + 1))
                at_least(dve, pv_done, (q - 2) * SLOTS + (G * b + G))
                dve.tensor_tensor(v[:, u, b, :], psD[1 - b][:, :], bv_bc[:, :], ALU.add).then_inc(v_ready, 1)

            def scores(p, t, b, g):
                at_least(dve, qk_done, t + 1)
                at_least(dve, bias_ready[b], p * G + (g + 1))
                at_least(dve, pt_done, t - 1)
                dve.tensor_tensor(s[:, g % 2, :, :], psS[g % 2][:, :, :], bias[:, b, HG * g:HG * g + HG, :],
                                  ALU.add).then_inc(score_ready, 1)
                at_least(dve, score_ready, t + 1)
                dve.tensor_reduce(mx[:, g % 2, :], s[:, g % 2, :, :], mybir.AxisListType.X, ALU.max).then_inc(max_done, 1)
                at_least(dve, max_done, t + 1)
                dve.tensor_scalar(nmx[:, g % 2, :], mx[:, g % 2, :], -1.0, None, ALU.mult).then_inc(nmax_ready, 1)

            def invert(t, i):
                at_least(dve, exp_done, t + 1)
                at_least(dve, prob_ready, t - 1)
                dve.reciprocal(rinv[:, i, :], sums[:, i, :]).then_inc(rinv_ready, 1)

            def negate_mask(q, b):
                at_least(dve, mask_in[b], (q + 1) * DMA)
                at_least(dve, bias_ready[b], q * G)
                dve.tensor_scalar(mneg[:, b, :], mask[:, b, :], LOWEST, None, ALU.mult).then_inc(neg_ready[b], 1)

            def context(q, b):
                at_least(dve, pv_done, q * SLOTS + (G * b + G))
                at_least(dve, o_done, q * 2 + b)
                split(dve, cT[0][:, :, :], cT[1][:, :, :], psC[:, :, :], ctx_hi, ctx_split, q * 2 + b)

            def add_residual(q, u, b):
                at_least(dve, o_done, q * 2 + (b + 1))
                at_least(dve, res_ready, q * 2 + (b + 1))
                at_least(dve, r_out[b], q * DMA)
                dve.tensor_tensor(rout[:, b, :], psD[0][:, :], xres[:, u, b, :], ALU.add).then_inc(r_ready, 1)

            def step(p, u, on):
                for n in range(SLOTS):
                    b, g = n // G, n % G
                    t = p * SLOTS + n
                    if on.attn and n or on.prev and n == 0:
                        invert(t - 1, (g - 1) % 2)
                    if n == 0 and on.attn:
                        split_q(p, 3)
                    if n == 1 and on.prev:
                        add_residual(p - 1, 1 - u, 0)
                    if n == 2 and on.proj:
                        add_bv(p + 1, 1 - u, 0)
                    if n == 5 and on.prev:
                        add_residual(p - 1, 1 - u, 1)
                    if on.attn:
                        scores(p, t, b, g)
                    if n == 0 and on.attn:
                        negate_mask(p, 1)
                    if n == 4 and on.proj:
                        negate_mask(p + 1, 0)
                    if n < 2 and on.turn or n == 1 and on.start:
                        norm.split(dve, p + 1, n)
                    if n == 4 and on.start:
                        dve.wait_ge(wo_hi, 1)
                        dve.tensor_tensor(wo[1][:, :, :], raw_o[:, :, :], wo[0][:, :, :].bitcast(F32),
                                          ALU.subtract).then_inc(wo_split, 1)
                    if n == 2 and on.prev:
                        context(p - 1, 1)
                    if n == 6 and on.attn:
                        context(p, 0)
                    if on.proj:
                        for gg in {3: (0, 1), 4: (2, 3)}.get(n, ()):
                            split_k(p + 1, gg)
                        for gg in {5: (0,), 6: (1,), 7: (2,)}.get(n, ()):
                            split_q(p + 1, gg)
                    if n == 5 and on.norm:
                        norm.statistics(dve, p + 2)
                    if n == 7 and on.norm:
                        norm.normalize(dve, p + 2, 0)
                    if n == 7 and on.proj:
                        add_bv(p + 1, 1 - u, 1)
                    if n == 7 and on.norm:
                        norm.normalize(dve, p + 2, 1)
                    if n in (2, 3) and on.tail:
                        for b in (2 * n - 4, 2 * n - 3):
                            second.statistics(dve, 0, 0, b)
                    if n == 3 and on.tail:
                        second.spread(dve, 0)
                    if n == 4 and on.tail:
                        dve.wait_ge(q_done, PAIRS * G)
                    if n >= 4 and on.tail:
                        second.normalize(dve, 0, 0, n - 4)
                    if n == 3 and not on.attn and on.prev:
                        second.split(dve, 0)

            run(dve, step)

        @block.tensor
        def _(pe):
            def three(out, stat, moving, start, stop):
                (sh, sl), (mh, ml) = stat, moving
                pe.matmul(out, sh, mh, start=start, stop=False)
                pe.matmul(out, sh, ml, start=False, stop=False)
                return pe.matmul(out, sl, mh, start=False, stop=stop)

            def qk(p, t, b, g):
                at_least(pe, score_ready, t - 1)
                if g == 0:
                    at_least(pe, kbd_in[b], (p + 1) * (HG * DMA))
                if b == 0:
                    at_least(pe, q_split, p * G + (g + 1))
                at = slice(b * P, (b + 1) * P)
                three(psS[g % 2][:, :, :], [x[:, g, at] for x in qT], [kbd[b][:, i, g, :, :] for i in range(2)],
                      True, True).then_inc(qk_done, 1)

            def transpose_p(t, i):
                at_least(pe, prob_ready, t + 1)
                at_least(pe, pt_copied, t - 1)
                for j in range(HG):
                    last = pe.transpose(psP[i][:, j, :], s[:, i, j, :], ident[:, :])
                last.then_inc(pt_done, 1)

            def pv(q, t, u, b, g):
                at_least(pe, pt_copied, t + 1)
                if g == 0:
                    at_least(pe, v_ready, q * 2 + (b + 1))
                    at_least(pe, ctx_split, q * 2 + b)
                for j in range(HG):
                    h = HG * g + j
                    last = pe.matmul(psC[HD * j:HD * j + HD, g, :], v[:, u, b, h * HD:(h + 1) * HD],
                                     pT[:, g % 2, j, :], start=True, stop=True, tile_position=(0, HD * j))
                last.then_inc(pv_done, 1)

            def project_v(q, b, chunks):
                if chunks[0] == 0:
                    at_least(pe, norm.x_split, q * 2 + (b + 1))
                at = slice(b * P, (b + 1) * P)
                for c in chunks:
                    last = three(psD[1 - b][:, :], [x[:, c, at] for x in xT], [m[:, c, :] for m in wv],
                                 c == 0, c == CH - 1)
                if chunks[-1] == CH - 1:
                    last.then_inc(v_done, 1)

            def project_t(q, g, wm, bank, done):
                if g == 0:
                    at_least(pe, norm.x_split, q * 2 + 2)
                for c in range(CH):
                    last = three(psD[bank][:, 0:2 * P], [m[:, c, g * P:(g + 1) * P] for m in wm],
                                 [x[:, c, :] for x in xT], c == 0, c == CH - 1)
                last.then_inc(done, 1)

            def project_o(q, b):
                at_least(pe, ctx_split, q * 2 + (b + 1))
                for c in range(CH):
                    last = three(psD[0][:, :], [x[:, c, :] for x in cT], [m[:, c, :] for m in wo], c == 0, c == CH - 1)
                last.then_inc(o_done, 1)

            def dense(p, n, on):
                q = p + 1
                if n == 0:
                    if on.turn:
                        norm.transpose(pe, q, 0)
                    if on.prev:
                        if on.attn:
                            at_least(pe, v_ready, p * 2 + 2)
                        else:
                            at_least(pe, r_ready, p * 2 - 2)
                        project_o(p - 1, 0)
                    if on.proj:
                        norm.transpose(pe, q, 1)
                if n == 1 and on.proj:
                    at_least(pe, q_copied, p * G + G)
                    project_v(q, 0, range(CH))
                if n == 2 and on.proj:
                    if on.prev:
                        at_least(pe, r_ready, p * 2 - 1)
                    else:
                        at_least(pe, v_ready, p * 2 + 2)
                    project_t(q, 0, wk, 0, k_done)
                    at_least(pe, v_ready, q * 2 + 1)
                    project_t(q, 1, wk, 1, k_done)
                if n == 3 and on.proj:
                    at_least(pe, k_copied, q * G + 1)
                    project_t(q, 2, wk, 0, k_done)
                    at_least(pe, k_copied, q * G + 2)
                    project_t(q, 3, wk, 1, k_done)
                if n == 4 and on.prev:
                    if on.proj:
                        at_least(pe, k_copied, q * G + 3)
                    else:
                        at_least(pe, r_ready, p * 2 - 1)
                    project_o(p - 1, 1)
                if n == 5 and on.proj:
                    at_least(pe, k_copied, q * G + 4)
                    project_t(q, 0, wq, 1, q_done)
                    if on.prev:
                        at_least(pe, r_ready, p * 2)
                    else:
                        at_least(pe, k_copied, q * G + 3)
                    project_t(q, 1, wq, 0, q_done)
                if n == 6 and on.proj:
                    at_least(pe, q_copied, q * G + 1)
                    project_t(q, 2, wq, 1, q_done)
                    at_least(pe, q_copied, q * G + 2)
                    project_v(q, 1, range(CH // 2))
                if n == 7 and on.proj:
                    project_v(q, 1, range(CH // 2, CH))
                    at_least(pe, q_copied, q * G + 3)
                    project_t(q, 3, wq, 1, q_done)
                    if on.start:
                        pe.wait_ge(wo_split, 1)

            def step(p, u, on):
                for n in range(SLOTS):
                    b, g = n // G, n % G
                    t = p * SLOTS + n
                    if on.attn:
                        qk(p, t, b, g)
                    dense(p, n, on)
                    if on.attn and n or on.prev and n == 0:
                        transpose_p(t - 1, (g - 1) % 2)
                    if n == 4 and on.tail:
                        pe.wait_ge(norm.xt_copied, B)
                        pe.wait_ge(q_copied, PAIRS * G)
                    if n >= 4 and on.tail:
                        second.transpose(pe, 0, n - 4)
                    if n == 1 and on.prev:
                        for g in (G - 2, G - 1):
                            pv(p - 1, t - 1 - G + g, 1 - u, 1, g)
                    if n in (3, 5, 7) and on.attn:
                        for m in (n - 3, n - 2):
                            pv(p, p * SLOTS + m, u, m // G, m % G)

            run(pe, step)


def feed_block(nc, d, norm, raws, gT, out):
    B, S, DM = d["x"].shape
    FF = d["W1"].shape[1]
    CH, J = DM // P, FF // P
    NB = norm.NB
    assert J == 16
    GROUPS, ROWS = B // NB, NB * P
    with ExitStack() as ctx:
        sb = lambda name, shape, dt=F32: ctx.enter_context(nc.sbuf_tensor(name, shape, dt))
        sem = lambda name: ctx.enter_context(nc.semaphore(name))
        w1 = [sb(f"w1_{n}", [P, CH, FF], F32R) for n in ("hi", "lo")]
        w2 = [sb(f"w2_{n}", [P, J, DM], F32R) for n in ("hi", "lo")]
        b1_c, b2_bc = sb("b1_c", [P, J]), sb("b2_bc", [P, DM])
        r, gf, hT, raw1, raw2 = norm.r, norm.gf, norm.hT, raws.raw1, raws.raw2
        psH = [ctx.enter_context(nc.psum_tensor(f"psH{i}", [P, ROWS], F32)) for i in range(2)]
        psY = [ctx.enter_context(nc.psum_tensor(f"psY{i}", [P, DM], F32)) for i in range(NB)]
        r_in, y_out, w_in, hn_ready, h_split, up_done = norm.r_in, norm.y_out, raws.arrived, norm.hn_ready, norm.h_split, norm.up_done
        b1_in, rows_in, w_hi, w_ready, b2_added = sem("b1_in"), sem("rows_in"), sem("w_hi"), sem("w_ready"), sem("b2_added")
        gelu_done, g_hi, g_split, down_done, y_ready = (
            sem("gelu_done"), sem("g_hi"), sem("g_split"), sem("down_done"), sem("y_ready"))
        block = ctx.enter_context(nc.Block())
        y_rows = out.rearrange("b s n -> s b n")
        NORM_AT = (6, 8, 10, 12)

        def run(eng, group):
            group(0, 0, True, True)
            with eng.Fori(0, (GROUPS - 2) // 2) as i:
                for u in range(2):
                    group(i * 2 + (1 + u), (1 + u) % 2, False, True)
            group(GROUPS - 1, (GROUPS - 1) % 2, False, False)

        @block.sync
        def _(sp):
            def group(n, u, first, more):
                if more:
                    norm.load(sp, n + 1, 1 - u)
                if first:
                    for j in range(2, J):
                        sp.wait_ge(w_ready, j - 1)
                        raws.load(sp, j)
                for b in range(NB):
                    at_least(sp, y_ready, n * NB + (b + 1))
                    sp.dma_start(y_rows[:, bass.ds(n * NB + b, 1), :], r[u][:, b, :]).then_inc(y_out[u], DMA)

            with nc.allow_non_contiguous_dma(reason="columns of biases"):
                sp.dma_start(b1_c[:, :], d["b1"].rearrange("(c p) -> p c", p=P)).then_inc(b1_in, DMA)
            sp.dma_start(b2_bc[:, :], d["b2"].rearrange("(a f) -> a f", a=1).to_broadcast([P, DM])).then_inc(rows_in, DMA)
            run(sp, group)
            for i in range(2):
                sp.wait_ge(y_out[i], GROUPS // 2 * NB * DMA)

        @block.gpsimd
        def _(pool):
            def add_b2(n, u):
                for b in range(NB):
                    at_least(pool, hn_ready, n * NB + (b + 1))
                    pool.tensor_tensor(r[u][:, b, :], r[u][:, b, :], b2_bc[:, :], ALU.add).then_inc(b2_added, 1)

            def group(n, u, first, more):
                if more:
                    norm.root(pool, n + 1)
                    add_b2(n + 1, 1 - u)

            pool.wait_ge(rows_in, DMA)
            add_b2(0, 0)
            run(pool, group)

        @block.scalar
        def _(act):
            def gelu(n, j):
                at_least(act, up_done, n * J + (j + 1))
                at_least(act, g_split, n * J + (j - 1))
                act.activation(gf[:, j % 2, :], psH[j % 2][:, :], ACT.Gelu_apprx_sigmoid,
                               bias=b1_c[:, j:j + 1]).then_inc(gelu_done, 1)

            def split_raw(j):
                act.wait_ge(w_in[j % 2], 2 * DMA * (j // 2 + 1))
                act.activation(w1[0][:, :, j * P:(j + 1) * P], raw1[:, j % 2, :, :], ACT.Copy).then_inc(w_hi, 1)
                act.activation(w2[0][:, j, :], raw2[:, j % 2, :], ACT.Copy).then_inc(w_hi, 1)

            def group(n, u, first, more):
                for j in range(J):
                    if first and j + 2 < J:
                        split_raw(j + 2)
                    gelu(n, j)
                    if more and j in NORM_AT:
                        norm.copy(act, n + 1, NORM_AT.index(j))

            split_raw(0)
            split_raw(1)
            act.wait_ge(b1_in, DMA)
            run(act, group)

        @block.vector
        def _(dve):
            def split_g(n, j):
                at_least(dve, gelu_done, n * J + (j + 1))
                at_least(dve, down_done, n * J + (j - 1))
                dve.tensor_copy(gT[0][:, j % 2, :], gf[:, j % 2, :]).then_inc(g_hi, 1)
                at_least(dve, g_hi, n * J + (j + 1))
                dve.tensor_tensor(gT[1][:, j % 2, :], gf[:, j % 2, :], gT[0][:, j % 2, :].bitcast(F32),
                                  ALU.subtract).then_inc(g_split, 1)

            def split_raw(j):
                dve.wait_ge(w_hi, 2 * j + 2)
                dve.tensor_tensor(w1[1][:, :, j * P:(j + 1) * P], raw1[:, j % 2, :, :],
                                  w1[0][:, :, j * P:(j + 1) * P].bitcast(F32), ALU.subtract)
                dve.tensor_tensor(w2[1][:, j, :], raw2[:, j % 2, :], w2[0][:, j, :].bitcast(F32),
                                  ALU.subtract).then_inc(w_ready, 1)

            def finish(n, u):
                at_least(dve, down_done, n * J + J)
                at_least(dve, b2_added, n * NB + NB)
                for b in range(NB):
                    dve.tensor_tensor(r[u][:, b, :], psY[b][:, :], r[u][:, b, :], ALU.add).then_inc(y_ready, 1)

            def group(n, u, first, more):
                for j in range(J):
                    if first and j + 2 < J:
                        split_raw(j + 2)
                    split_g(n, j)
                    if more and 1 <= j <= NB:
                        norm.statistics(dve, n + 1, 1 - u, j - 1)
                    if more and j == NB:
                        norm.spread(dve, n + 1)
                    if more and j + 1 in NORM_AT:
                        norm.normalize(dve, n + 1, 1 - u, NORM_AT.index(j + 1))
                if more:
                    norm.split(dve, n + 1)
                finish(n, u)

            split_raw(0)
            split_raw(1)
            run(dve, group)

        @block.tensor
        def _(pe):
            def three(out_ap, stat, moving, start, stop):
                (sh, sl), (mh, ml) = stat, moving
                pe.matmul(out_ap, sh, mh, start=start, stop=False)
                pe.matmul(out_ap, sh, ml, start=False, stop=False)
                return pe.matmul(out_ap, sl, mh, start=False, stop=stop)

            def up(n, j, first):
                if first:
                    pe.wait_ge(w_ready, j + 1)
                at_least(pe, gelu_done, n * J + (j - 1))
                for c in range(CH):
                    if j == 0:
                        at_least(pe, h_split, n * CH + (c + 1))
                    last = three(psH[j % 2][:, :], [m[:, c, j * P:(j + 1) * P] for m in w1],
                                 [x[:, c, :] for x in hT], c == 0, c == CH - 1)
                last.then_inc(up_done, 1)

            def down(n, j):
                at_least(pe, g_split, n * J + (j + 1))
                for b in range(NB):
                    if j == 0:
                        at_least(pe, y_ready, (n - 1) * NB + (b + 1))
                    last = three(psY[b][:, :], [x[:, j % 2, b * P:(b + 1) * P] for x in gT],
                                 [m[:, j, :] for m in w2], j == 0, j == J - 1)
                last.then_inc(down_done, 1)

            def group(n, u, first, more):
                for j in range(J):
                    up(n, j, first)
                    if more and j in NORM_AT:
                        norm.transpose(pe, n + 1, NORM_AT.index(j))
                    if j:
                        down(n, j - 1)
                down(n, J - 1)

            run(pe, group)


def layer(nc, d, out):
    B, S, DM = d["x"].shape
    CH, H = DM // P, d["bias"].shape[1]
    assert S == P and DM == 4 * P and H == 16 and B % 4 == 0
    resid = nc.dram_tensor("resid", [B, S, DM], F32, kind="Internal").ap()
    ada_rows = nc.dram_tensor("ada_rows", [B, 2 * DM], F32, kind="Internal").ap()
    with ExitStack() as whole:
        shared = lambda name, shape, dt=F32: whole.enter_context(nc.sbuf_tensor(name, shape, dt))
        ident = shared("ident", [P, P])
        wo = [shared(f"wo_{part}", [P, CH, DM], F32R) for part in ("hi", "lo")]
        raw_o = shared("raw_o", [P, CH, DM])
        turn = [whole.enter_context(nc.psum_tensor(f"turn{i}", [P, CH, P], F32)) for i in range(2)]
        with ExitStack() as used_first:
            w = [[used_first.enter_context(nc.sbuf_tensor(f"w{n}_{part}", [P, CH, DM], F32R)) for part in ("hi", "lo")]
                 for n in "qkv"] + [wo]
        second = SecondNorm(nc, whole, resid, ident, turn, 4)
        raws = RawWeights(nc, whole, d, raw_o)
        with ExitStack() as ctx:
            sb = lambda name, shape, dt=F32: ctx.enter_context(nc.sbuf_tensor(name, shape, dt))
            bq_s, bk_c, bv_bc = sb("bq_s", [P, CH]), sb("bk_c", [P, CH]), sb("bv_bc", [P, DM])
            kbd = [sb(f"kbd{b}", [P, 2, H // 4, 4, P], F32R) for b in range(2)]
            wo_in = ctx.enter_context(nc.semaphore("wo_in"))
            psD = [ctx.enter_context(nc.psum_tensor("psD0", [P, DM], F32)), turn[1][:, :, :].rearrange("p c k -> p (c k)")]
            first = FirstNorm(nc, ctx, d["x"], ident, turn[0])
            setup_block(nc, d, w, first, ada_rows, bq_s, bk_c, bv_bc, kbd, raw_o, wo_in)
            attention_block(nc, d, w, first, ada_rows, resid, psD, bq_s, bk_c, bv_bc, kbd, raw_o, wo_in, second, raws)
        feed_block(nc, d, second, raws, [wo[0][:, 0:2, :], wo[0][:, 2:4, :]], out)


_INS = {"x": "x", "t": "itok_B_34_63", "bias": "fside_Bx16xSxS_0", "mask": "mask_Bx1xSxS_bk0"} | {
    n: f"L0_cond_{n}" for n in ("W_ada", "b_ada", "Wq", "bq", "Wk", "bk", "Wv", "bv", "Wo", "bo",
                                "W1", "b1", "W2", "b2", "g2", "beta2")}


def kernel(**inputs):
    import concourse.bacc as bacc
    from concourse.bass_utils import run_bass_kernel_spmd

    nc = bacc.Bacc("TRN2", target_bir_lowering=False, num_devices=1)
    arrays, d = {}, {}
    for short, name in _INS.items():
        a = np.ascontiguousarray(inputs[name])
        arrays[f"in_{short}"] = a
    half = arrays["in_x"].shape[2] // 2
    arrays["in_freqs"] = np.exp(np.arange(half, dtype=np.float32) * np.float32(-math.log(10000.0) / (half - 1)))
    for name, a in arrays.items():
        d[name[3:]] = nc.dram_tensor(name, a.shape, mybir.dt.from_np(a.dtype), kind="ExternalInput").ap()
    out = nc.dram_tensor("out", arrays["in_x"].shape, F32, kind="ExternalOutput").ap()
    layer(nc, d, out)
    r = run_bass_kernel_spmd(nc, [arrays], core_ids=[0])
    return r.results[0]["out"]
```
